# Optimizing a Trainium2 kernel written in Bass

```python
import numpy as np
import jax
import jax.numpy as jnp

def _softmax(x, axis=-1):
    return jax.nn.softmax(x, axis=axis)

def _gelu(x):
    return jax.nn.gelu(x, approximate=True)

def _silu(x):
    return jax.nn.silu(x)

def _sigmoid(x):
    return jax.nn.sigmoid(x)

def _layernorm(x, axis=-1, eps=1e-05):
    m = jnp.mean(x, axis=axis, keepdims=True)
    v = jnp.var(x, axis=axis, keepdims=True)
    return (x - m) / jnp.sqrt(v + eps)

def _scatter_add(tgt, idx, src, axis=0):
    return tgt.at[idx].add(src)

def _segment_sum(src, seg, n):
    return jax.ops.segment_sum(src, seg, n)
kernel_name = 'mk_adj_resnorm_d1_adj_r2_401249'

def setup_inputs(seed: int=0):
    np.random.seed(seed)
    _w = jnp.asarray

    def _rec_inputs():
        import jax
        import jax.numpy as jnp
        _gk = jax.random.key(seed)
        x = -0.0004039 + 1 * jax.random.normal(jax.random.fold_in(_gk, 1), (128, 128, 384), jnp.float32)
        _a = jax.random.bernoulli(jax.random.fold_in(_gk, 2), 0.125, (128, 128, 128))
        _af = _a.astype(jnp.float32)
        adj = _af
        return (x, adj)
    x, adj = _rec_inputs()

    def _L0_gnn_setup():
        import jax, jax.numpy as jnp
        import numpy as np
        B, S, H, L = (32, 256, 384, 2)

        def _layer_norm(z, a, b, eps=0.001):
            mu = jnp.mean(z, axis=-1, keepdims=True)
            sigma = jnp.std(z, axis=-1, keepdims=True, ddof=1)
            return (z - mu) / (sigma + eps) * a + b
        key = jax.random.key(seed)
        ks = jax.random.split(key, 6)
        hidden_state = jax.random.normal(ks[0], (B, S, H), dtype=jnp.float32)
        adjacency_matrix = (jax.random.uniform(ks[1], (B, S, S)) < 0.2).astype(jnp.float32)
        W_left = 0.05 * jax.random.normal(ks[2], (L, H, H), dtype=jnp.float32)
        W_right = 0.05 * jax.random.normal(ks[3], (L, H, H), dtype=jnp.float32)
        W_lin = 0.05 * jax.random.normal(ks[4], (L, H, H), dtype=jnp.float32)
        b_lin = jnp.zeros((L, H), dtype=jnp.float32)
        ln_a = jnp.ones((L, H), dtype=jnp.float32)
        ln_b = jnp.zeros((L, H), dtype=jnp.float32)
        return {'hidden_state': hidden_state, 'adjacency_matrix': adjacency_matrix, 'W_left': W_left, 'W_right': W_right, 'W_lin': W_lin, 'b_lin': b_lin, 'ln_a': ln_a, 'ln_b': ln_b}
    _L0_gnn_all = _L0_gnn_setup()
    _L0_gnn_in = {k: v for k, v in _L0_gnn_all.items() if k in ('W_left', 'W_right', 'W_lin', 'b_lin', 'ln_a', 'ln_b')}
    del _L0_gnn_all
    return {'x': x, 'adj': adj, 'L0_gnn_W_left': _L0_gnn_in['W_left'], 'L0_gnn_W_right': _L0_gnn_in['W_right'], 'L0_gnn_W_lin': _L0_gnn_in['W_lin'], 'L0_gnn_b_lin': _L0_gnn_in['b_lin'], 'L0_gnn_ln_a': _L0_gnn_in['ln_a'], 'L0_gnn_ln_b': _L0_gnn_in['ln_b']}

def reference(x, adj, L0_gnn_W_left, L0_gnn_W_right, L0_gnn_W_lin, L0_gnn_b_lin, L0_gnn_ln_a, L0_gnn_ln_b):
    import jax
    import jax.numpy as jnp

    def _L0_gnn_ref(hidden_state, adjacency_matrix, W_left, W_right, W_lin, b_lin, ln_a, ln_b):
        import jax, jax.numpy as jnp
        import numpy as np
        B, S, H, L = (32, 256, 384, 2)

        def _layer_norm(z, a, b, eps=0.001):
            mu = jnp.mean(z, axis=-1, keepdims=True)
            sigma = jnp.std(z, axis=-1, keepdims=True, ddof=1)
            return (z - mu) / (sigma + eps) * a + b
        temper = float(np.sqrt(H))
        adj = adjacency_matrix
        adj_tri = jnp.triu(adj, k=1)
        diag_mask = jnp.triu(adj, k=0) - adj_tri
        h = hidden_state
        for l in range(L):
            m_left = jnp.einsum('bsh,oh->bso', h, W_left[l])
            m_right = jnp.einsum('bsh,oh->bso', h, W_right[l])
            u_left = jnp.einsum('bih,bjh->bij', h, m_left) / temper
            u_right = jnp.einsum('bih,bjh->bij', h, m_right) / temper
            u = u_left * adj_tri + u_left * diag_mask + u_right * jnp.swapaxes(adj_tri, 1, 2)
            delta_exp_u = jnp.exp(u) * adj
            attention = delta_exp_u / (jnp.sum(delta_exp_u, axis=2, keepdims=True) + 1e-10)
            h_lin = jnp.einsum('bsh,oh->bso', h, W_lin[l]) + b_lin[l]
            ctx = jnp.matmul(attention, h_lin)
            h = jax.nn.relu(_layer_norm(ctx, ln_a[l], ln_b[l]))
        return h
    x = _layernorm(x + _L0_gnn_ref(x, adj, L0_gnn_W_left, L0_gnn_W_right, L0_gnn_W_lin, L0_gnn_b_lin, L0_gnn_ln_a, L0_gnn_ln_b), axis=-1)
    return x

_drawn_inputs = setup_inputs


def setup_inputs(seed=0):
    import zlib

    import numpy as np

    out = dict(_drawn_inputs(seed))
    spreads = {'L0_gnn_b_lin': (0.0, 0.1), 'L0_gnn_ln_a': (1.0, 0.2), 'L0_gnn_ln_b': (0.0, 0.1)}
    factors = {}
    for name, (base, spread) in spreads.items():
        noise = np.random.default_rng([zlib.crc32(name.encode()), seed]).standard_normal(out[name].shape)
        drawn = base * np.exp(spread * noise) if base else spread * noise
        out[name] = jnp.asarray(drawn.astype(out[name].dtype))
    for name, factor in factors.items():
        out[name] = (out[name] * factor).astype(out[name].dtype)
    return out
```

```python
import numpy as np
import concourse.bass as bass
from concourse import mybir
from contextlib import ExitStack


def gnn_attention_resnorm_kernel(nc, x_nat, x_t, adj_pair, w_side, w_lin_t, rows, cols, out):
    fp32, fp32r, i32 = mybir.dt.float32, mybir.dt.float32r, mybir.dt.int32
    ALU, ACT = mybir.AluOpType, mybir.ActivationFunctionType

    P = 128
    B, S, H = x_nat.shape
    L = w_lin_t.shape[0]
    QB = 4
    NQ = B // QB
    HC = H // P
    QS = QB * S
    NG = 2 * HC
    HX = H + 2
    assert S == P and L == 2 and B % QB == 0 and H % P == 0 and QS == 512

    INV_TEMPER = float(1.0 / np.float32(np.sqrt(H)))
    LN_EPS, SUM_EPS, OUT_EPS = 1e-3, 1e-10, 1e-5
    DDOF = float(np.sqrt(H / (H - 1.0)))

    x_q = x_nat.rearrange("(q b) s h -> q s b h", b=QB)
    out_q = out.rearrange("(q b) s h -> q s b h", b=QB)

    FIRST_FULL, END_FULL = 3, NQ - 1
    END = NQ + 3

    ctx = ExitStack()
    with ctx:
        def sb(name, shape, dt=fp32):
            return ctx.enter_context(nc.sbuf_tensor(name, shape, dt))

        def sem(name):
            return ctx.enter_context(nc.semaphore(name))

        def sem_pair(name):
            return [sem(f"{name}{l}") for l in range(L)]

        ws_hi = sb("ws_hi", [P, L, 2, HC, H], fp32r)
        ws_lo = sb("ws_lo", [P, L, 2, HC, H], fp32r)
        wl_hi = sb("wl_hi", [P, L, HC, H], fp32r)
        wl_lo = sb("wl_lo", [P, L, HC, H], fp32r)
        row_tab = sb("row_tab", [P, 4, H])
        b_lin = [row_tab[:, 0, :], row_tab[:, 1, :]]
        a_row, b_row = row_tab[:, 2, :], row_tab[:, 3, :]
        col_tab = sb("col_tab", [P, 2, HC])
        ident = sb("ident", [P, P])
        use_right = sb("use_right", [P, QB, S], i32)
        halves = sb("halves", [P, 2, QB])

        h32 = [sb(f"h32_{l}", [P, HC, QS]) for l in range(L)]
        h_hi = [sb(f"h_hi{l}", [P, HC, QS], fp32r) for l in range(L)]
        h_lo = [sb(f"h_lo{l}", [P, HC, QS], fp32r) for l in range(L)]
        lin_hi = [sb(f"lin_hi{l}", [P, QB, HX], fp32r) for l in range(L)]
        lin_lo = [sb(f"lin_lo{l}", [P, QB, HX], fp32r) for l in range(L)]
        p_hi = [sb(f"p_hi{l}", [P, QS], fp32r) for l in range(L)]
        p_lo = [sb(f"p_lo{l}", [P, QS], fp32r) for l in range(L)]
        y = [sb(f"y{l}", [P, QB, HX]) for l in range(L)]
        masks = [sb(f"masks{l}", [P, 2, QS]) for l in range(L)]
        stat = [sb(f"stat{l}", [P, QB, 6]) for l in range(L)]
        mv = [sb(f"mv{l}", [P, QB, 2]) for l in range(L)]
        sd = [sb(f"sd{l}", [P, QB]) for l in range(L)]
        eps_s = [sb(f"eps_s{l}", [P, QB]) for l in range(L)]
        den = [sb(f"den{l}", [P, QB]) for l in range(L)]
        k_ln = [sb(f"k_ln{l}", [P, QB]) for l in range(L)]
        nb_ln = [sb(f"nb_ln{l}", [P, QB]) for l in range(L)]

        g_hi = sb("g_hi", [P, HC, QB, 2 * S], fp32r)
        g_lo = sb("g_lo", [P, HC, QB, 2 * S], fp32r)
        lin32 = sb("lin32", [P, QB, H])
        score = sb("score", [P, QS])
        p32 = sb("p32", [P, QS])
        adj_nat = sb("adj_nat", [P, QS])
        x_res = sb("x_res", [P, QB, H])
        stat_o = sb("stat_o", [P, QB, 6])
        mv_o = sb("mv_o", [P, QB, 2])
        var_o = sb("var_o", [P, QB])
        rstd_o = sb("rstd_o", [P, QB])
        nb_o = sb("nb_o", [P, QB])
        o_sb = sb("o_sb", [P, QB, H])

        ps_g = ctx.enter_context(nc.psum_tensor("ps_g", [P, 2, QB, S], fp32))
        ps_u = ctx.enter_context(nc.psum_tensor("ps_u", [P, QB, 2 * S], fp32))
        ps_h = ctx.enter_context(nc.psum_tensor("ps_h", [P, 2, 512], fp32))
        ps_c = ctx.enter_context(nc.psum_tensor("ps_c", [P, 2, 512], fp32))

        def stage(t):
            return t[:, :, :].rearrange("p a b -> p (a b)")[:, 0:HC * H]

        raw_w = [[stage(h32[1]), stage(lin32), stage(x_res)], [stage(y[0]), stage(y[1]), stage(o_sb)]]

        w_loaded = [sem(f"w_loaded{n}") for n in range(3 * L)]
        tab_loaded = sem("tab_loaded")
        col_loaded = sem("col_loaded")
        w_hi_done = sem("w_hi_done")
        w_lo_done = sem("w_lo_done")
        const_step = sem("const_step")
        const_done = sem("const_done")
        pads_done = sem("pads_done")
        xt_loaded = sem("xt_loaded")
        adj_loaded = sem("adj_loaded")
        masks_moved = sem("masks_moved")
        xres_loaded = sem("xres_loaded")
        out_stored = sem("out_stored")
        g_done, g_hi_done, g_lo_done = sem_pair("g_done"), sem_pair("g_hi_done"), sem_pair("g_lo_done")
        lin_done, lin_sum_done = sem_pair("lin_done"), sem_pair("lin_sum_done")
        lin_hi_done, lin_lo_done = sem_pair("lin_hi_done"), sem_pair("lin_lo_done")
        u_done, u_sel_done, u_mul_done = sem_pair("u_done"), sem_pair("u_sel_done"), sem_pair("u_mul_done")
        exp_done, p_full_done = sem_pair("exp_done"), sem_pair("p_full_done")
        p_hi_done, p_lo_done = sem_pair("p_hi_done"), sem_pair("p_lo_done")
        ctx_done, y_done = sem_pair("ctx_done"), sem_pair("y_done")
        h_hi_done, h_lo_done = sem_pair("h_hi_done"), sem_pair("h_lo_done")
        stats_done, mv_done, sd_done = sem_pair("stats_done"), sem_pair("mv_done"), sem_pair("sd_done")
        ln_step, z_done = sem_pair("ln_step"), sem_pair("z_done")
        tr_done = sem("tr_done")
        relu_done = sem("relu_done")
        mask_step = sem("mask_step")
        mask_done = sem("mask_done")
        aff_mul_done = sem("aff_mul_done")
        aff_done = sem("aff_done")
        res_done = sem("res_done")
        stats_o_done = sem("stats_o_done")
        mv_o_done = sem("mv_o_done")
        var_o_done = sem("var_o_done")
        rstd_o_done = sem("rstd_o_done")
        nb_o_done = sem("nb_o_done")
        norm_done = sem("norm_done")

        block = ctx.enter_context(nc.Block())

        def wait(eng, s, n):
            if isinstance(n, int) and n <= 0:
                return
            eng.wait_ge(s, n)

        def wait_alone(eng, s, n):
            if not isinstance(n, int):
                eng.compute_val(n)
            eng.wait_ge(const_done, 1)
            wait(eng, s, n)

        def has(q):
            return not isinstance(q, int) or 0 <= q < NQ

        def iterations(eng, body):
            for t in range(FIRST_FULL):
                body(t)
            with eng.Fori(FIRST_FULL, END_FULL) as t:
                body(t)
            for t in range(END_FULL, END):
                body(t)

        def prior(l, q):
            if l == 0:
                return 1, q - 2
            return (0, q + 1) if has(q + 1) else (1, q - 1)

        @block.sync
        def _(sp):
            sp.dma_start(h32[0][:, :, :].rearrange("p c n -> p (c n)"), x_t[0, :, :]).then_inc(xt_loaded, 16)
            for n in range(3 * L):
                l, kind = n // 3, n % 3
                src = w_side[l, kind] if kind < 2 else w_lin_t[l]
                sp.dma_start(raw_w[l][kind].rearrange("p (c n) -> p c n", c=HC),
                             src.rearrange("(c p) n -> p c n", p=P)).then_inc(w_loaded[n], 16)
                if n == 0:
                    sp.dma_start(row_tab[:, :, :], rows).then_inc(tab_loaded, 16)
                    sp.dma_start(col_tab[:, :, :], cols).then_inc(col_loaded, 16)

            def body(t):
                if has(t - 1):
                    wait(sp, p_full_done[1], t - 1)
                    wait(sp, mask_done, t)
                    sp.dma_start(masks[1][:, :, :], masks[0][:, :, :]).then_inc(masks_moved, 16)
                if has(t):
                    wait(sp, masks_moved, 16 * t)
                    wait(sp, p_full_done[0], t)
                    sp.dma_start(masks[0][:, 1, :], adj_pair[t, :, 1, :]).then_inc(adj_loaded, 16)
                    sp.dma_start(adj_nat[:, :], adj_pair[t, :, 0, :]).then_inc(adj_loaded, 16)
                if has(t - 2):
                    wait(sp, res_done, QB * (t - 2))
                    if isinstance(t, int) and t == 2:
                        wait(sp, w_lo_done, 3 * L)
                    sp.dma_start(x_res[:, :, :], x_q[t - 2, :, :, :]).then_inc(xres_loaded, 16)
                if has(t) and has(t + 1):
                    wait(sp, h_hi_done[0], t + 1)
                    wait(sp, h_lo_done[0], t + 1)
                    sp.dma_start(h32[0][:, :, :].rearrange("p c n -> p (c n)"),
                                 x_t[t + 1, :, :]).then_inc(xt_loaded, 16)
                if has(t - 3):
                    wait(sp, norm_done, t - 2)
                    sp.dma_start(out_q[t - 3, :, :, :], o_sb[:, :, :]).then_inc(out_stored, 16)

            iterations(sp, body)
            sp.wait_ge(out_stored, 16 * NQ)

        @block.tensor
        def _(pe):
            def three_passes(out_ap, terms):
                n = len(terms)
                for i, (a_hi, a_lo, b_hi, b_lo) in enumerate(terms):
                    pe.matmul(out_ap, a_hi, b_hi, start=(i == 0), stop=False)
                    pe.matmul(out_ap, a_hi, b_lo, start=False, stop=False)
                    last = pe.matmul(out_ap, a_lo, b_hi, start=False, stop=(i == n - 1))
                return last

            def project_sides(l, q):
                wait(pe, h_hi_done[l], q + 1)
                wait(pe, h_lo_done[l], q + 1)
                if isinstance(q, int) and q == 0:
                    pe.wait_ge(w_lo_done, 3 * l + 2)
                for j in range(NG):
                    side, m = j % 2, j // 2
                    if j >= 2:
                        wait(pe, g_lo_done[l], NG * q + j - 1)
                    three_passes(ps_g[:, j % 2, :, :].rearrange("p b s -> p (b s)"),
                                 [(ws_hi[:, l, side, c, m * P:(m + 1) * P], ws_lo[:, l, side, c, m * P:(m + 1) * P],
                                   h_hi[l][:, c, :], h_lo[l][:, c, :]) for c in range(HC)]).then_inc(g_done[l], 1)

            def linear(l, q):
                if isinstance(q, int) and q == 0:
                    pe.wait_ge(w_lo_done, 3 * l + 3)
                for b in range(QB):
                    if b < 2:
                        pl, pq = prior(l, q)
                        wait(pe, lin_sum_done[pl], QB * pq + 3 + b)
                    else:
                        wait(pe, lin_sum_done[l], QB * q + b - 1)
                    three_passes(ps_h[:, b % 2, 0:H],
                                 [(h_hi[l][:, c, b * S:(b + 1) * S], h_lo[l][:, c, b * S:(b + 1) * S],
                                   wl_hi[:, l, c, :], wl_lo[:, l, c, :]) for c in range(HC)]).then_inc(lin_done[l], 1)

            def scores(l, q):
                wait(pe, g_lo_done[l], NG * (q + 1))
                pl, pq = prior(l, q)
                wait(pe, u_mul_done[pl], pq + 1)
                for b in range(QB):
                    three_passes(ps_u[:, b, :],
                                 [(h_hi[l][:, c, b * S:(b + 1) * S], h_lo[l][:, c, b * S:(b + 1) * S],
                                   g_hi[:, c, b, :], g_lo[:, c, b, :]) for c in range(HC)]).then_inc(u_done[l], 1)

            def context(l, q):
                wait(pe, p_lo_done[l], q + 1)
                wait(pe, lin_lo_done[l], q + 1)
                for b in range(QB):
                    if b < 2 and l == 1:
                        if has(q + 1):
                            wait(pe, relu_done, HC * (q + 2))
                        else:
                            wait(pe, y_done[1], QB * q)
                    elif b < 2:
                        wait(pe, y_done[1], QB * (q - 2) + 3 + b)
                        if isinstance(q, int) and q == 1:
                            wait(pe, relu_done, HC)
                    else:
                        wait(pe, y_done[l], QB * q + b - 1)
                    three_passes(ps_c[:, b % 2, 0:HX],
                                 [(p_hi[l][:, b * S:(b + 1) * S], p_lo[l][:, b * S:(b + 1) * S],
                                   lin_hi[l][:, b, :], lin_lo[l][:, b, :])]).then_inc(ctx_done[l], 1)

            def transposes(q):
                wait(pe, z_done[0], QB * (q + 1))
                for c in range(HC):
                    if c >= 2:
                        wait(pe, relu_done, HC * q + c - 1)
                    for b in range(QB):
                        last = pe.transpose(ps_c[:, c % 2, b * S:(b + 1) * S], y[0][:, b, c * P:(c + 1) * P],
                                            ident[:, :])
                    last.then_inc(tr_done, 1)

            def body(t):
                if has(t):
                    project_sides(0, t)
                if has(t - 1):
                    transposes(t - 1)
                if has(t):
                    linear(0, t)
                    scores(0, t)
                if has(t - 2):
                    context(1, t - 2)
                if has(t - 1):
                    project_sides(1, t - 1)
                    linear(1, t - 1)
                    scores(1, t - 1)
                if has(t):
                    context(0, t)

            pe.wait_ge(const_done, 1)
            pe.wait_ge(pads_done, 1)
            iterations(pe, body)

        @block.scalar
        def _(act):
            for n in range(3 * L):
                l, kind = n // 3, n % 3
                act.wait_ge(w_loaded[n], 16)
                dst = ws_hi[:, l, kind, :, :] if kind < 2 else wl_hi[:, l, :, :]
                nc.scalar.activation(dst.rearrange("p c n -> p (c n)"), raw_w[l][kind], ACT.Copy).then_inc(w_hi_done, 1)
            act.wait_ge(col_loaded, 16)

            def sides_hi(l, q, js):
                for j in js:
                    side, m = j % 2, j // 2
                    if j == 0:
                        pl, pq = prior(l, q)
                        wait(act, u_done[pl], QB * (pq + 1))
                    wait(act, g_done[l], NG * q + j + 1)
                    nc.scalar.activation(g_hi[:, m, :, side * S:(side + 1) * S], ps_g[:, j % 2, :, :],
                                         ACT.Copy).then_inc(g_hi_done[l], 1)

            def relu_affine(q):
                wait(act, h_hi_done[1], q)
                wait(act, h_lo_done[1], q)
                if isinstance(q, int) and q == 0:
                    act.wait_ge(w_lo_done, 3 * L)
                for c in range(HC):
                    wait(act, tr_done, HC * q + c + 1)
                    nc.scalar.activation(h32[1][:, c, :], ps_c[:, c % 2, :], ACT.Relu, bias=col_tab[:, 1, c:c + 1],
                                         scale=col_tab[:, 0, c:c + 1]).then_inc(relu_done, 1)

            def linear_hi(l, q):
                wait(act, lin_sum_done[l], QB * (q + 1))
                wait(act, ctx_done[l], QB * q)
                nc.scalar.activation(lin_hi[l][:, :, 0:H], lin32[:, :, :], ACT.Copy).then_inc(lin_hi_done[l], 1)

            def take_context(l, q):
                if l == 0:
                    wait(act, tr_done, HC * q)
                else:
                    wait(act, norm_done, q)
                if isinstance(q, int) and q == 0:
                    act.wait_ge(w_lo_done, 3 * L)
                for b in range(QB):
                    wait(act, ctx_done[l], QB * q + b + 1)
                    nc.scalar.activation(y[l][:, b, 0:H + 1], ps_c[:, b % 2, 0:H + 1],
                                         ACT.Copy).then_inc(y_done[l], 1)

            def exponentials(l, q):
                wait(act, u_mul_done[l], q + 1)
                nc.scalar.activation(score[:, :], score[:, :], ACT.Exp, scale=INV_TEMPER).then_inc(exp_done[l], 1)

            def output_norm(q):
                wait(act, nb_o_done, q + 1)
                wait(act, out_stored, 16 * q)
                for b in range(QB):
                    last = nc.scalar.activation(o_sb[:, b, :], y[1][:, b, 0:H], ACT.Identity,
                                                bias=nb_o[:, b:b + 1], scale=rstd_o[:, b:b + 1])
                last.then_inc(norm_done, 1)

            def body(t):
                if has(t):
                    sides_hi(0, t, range(2))
                if has(t - 3):
                    output_norm(t - 3)
                if has(t):
                    sides_hi(0, t, range(2, NG))
                if has(t - 1):
                    relu_affine(t - 1)
                if has(t):
                    linear_hi(0, t)
                if has(t - 2):
                    take_context(1, t - 2)
                if has(t):
                    exponentials(0, t)
                if has(t - 1):
                    sides_hi(1, t - 1, range(NG))
                    linear_hi(1, t - 1)
                if has(t):
                    take_context(0, t)
                if has(t - 1):
                    exponentials(1, t - 1)

            iterations(act, body)

        @block.vector
        def _(dve):
            def split_h(l, q):
                if l == 0:
                    wait(dve, xt_loaded, 16 * (q + 1))
                else:
                    wait(dve, relu_done, HC * (q + 1))
                wait(dve, u_done[l], QB * q)
                nc.vector.tensor_copy(h_hi[l][:, :, :], h32[l][:, :, :]).then_inc(h_hi_done[l], 1)

            def sides_lo(l, q, js):
                for j in js:
                    side, m = j % 2, j // 2
                    wait(dve, g_hi_done[l], NG * q + j + 1)
                    cols_j = slice(side * S, (side + 1) * S)
                    nc.vector.tensor_tensor(g_lo[:, m, :, cols_j], ps_g[:, j % 2, :, :],
                                            g_hi[:, m, :, cols_j].bitcast(fp32), ALU.subtract).then_inc(g_lo_done[l], 1)

            def linear_sum(l, q, bs):
                for b in bs:
                    if b == 0:
                        pl, pq = prior(l, q)
                        wait(dve, lin_hi_done[pl], pq + 1)
                        wait(dve, lin_lo_done[pl], pq + 1)
                    wait(dve, lin_done[l], QB * q + b + 1)
                    nc.vector.tensor_tensor(lin32[:, b, :], ps_h[:, b % 2, 0:H], b_lin[l],
                                            ALU.add).then_inc(lin_sum_done[l], 1)

            def masked_scores(l, q):
                wait_alone(dve, u_done[l], QB * (q + 1))
                nc.vector.copy_predicated(ps_u[:, :, 0:S], use_right[:, :, :],
                                          ps_u[:, :, S:2 * S]).then_inc(u_sel_done[l], 1)
                wait(dve, u_sel_done[l], q + 1)
                if l == 0:
                    wait(dve, mask_done, q + 1)
                else:
                    wait(dve, masks_moved, 16 * (q + 1))
                nc.vector.tensor_tensor(score[:, :].rearrange("p (b s) -> p b s", b=QB), ps_u[:, :, 0:S],
                                        masks[l][:, 0, :].rearrange("p (b s) -> p b s", b=QB),
                                        ALU.mult).then_inc(u_mul_done[l], 1)

            def attention(l, q):
                wait(dve, exp_done[l], q + 1)
                nc.vector.tensor_tensor(p32[:, :], score[:, :], masks[l][:, 1, :], ALU.mult).then_inc(p_full_done[l], 1)
                wait(dve, p_full_done[l], q + 1)
                wait(dve, ctx_done[l], QB * q)
                nc.vector.tensor_copy(p_hi[l][:, :], p32[:, :]).then_inc(p_hi_done[l], 1)
                wait(dve, p_hi_done[l], q + 1)
                nc.vector.tensor_tensor(p_lo[l][:, :], p32[:, :], p_hi[l][:, :].bitcast(fp32),
                                        ALU.subtract).then_inc(p_lo_done[l], 1)

            def layer_stats(l, q):
                for b in range(QB):
                    wait(dve, y_done[l], QB * q + b + 1)
                    nc.vector.bn_stats(stat[l][:, b, :], y[l][:, b, 0:H]).then_inc(stats_done[l], 1)
                nc.vector.tensor_scalar(eps_s[l][:, :], y[l][:, :, H], LN_EPS, LN_EPS * SUM_EPS,
                                        ALU.mult, ALU.add).then_inc(ln_step[l], 1)
                for b in range(QB):
                    wait_alone(dve, stats_done[l], QB * q + b + 1)
                    last = nc.vector.bn_aggr(mv[l][:, b, :], stat[l][:, b, :])
                last.then_inc(mv_done[l], 1)

            def layer_norm(l, q):
                wait(dve, sd_done[l], q + 1)
                wait(dve, ln_step[l], 4 * q + 1)
                nc.vector.scalar_tensor_tensor(den[l][:, :], sd[l][:, :], DDOF, eps_s[l][:, :],
                                               ALU.mult, ALU.add).then_inc(ln_step[l], 1)
                wait(dve, ln_step[l], 4 * q + 2)
                nc.vector.reciprocal(k_ln[l][:, :], den[l][:, :]).then_inc(ln_step[l], 1)
                wait(dve, ln_step[l], 4 * q + 3)
                nc.vector.scalar_tensor_tensor(nb_ln[l][:, :], mv[l][:, :, 0], -1.0, k_ln[l][:, :],
                                               ALU.mult, ALU.mult).then_inc(ln_step[l], 1)
                wait(dve, ln_step[l], 4 * q + 4)
                for b in range(QB):
                    nc.vector.tensor_scalar(y[l][:, b, 0:H], y[l][:, b, 0:H], k_ln[l][:, b:b + 1],
                                            nb_ln[l][:, b:b + 1], ALU.mult, ALU.add).then_inc(z_done[l], 1)

            def residual(q):
                wait(dve, xres_loaded, 16 * (q + 1))
                for b in range(QB):
                    wait(dve, aff_done, QB * q + b + 1)
                    nc.vector.scalar_tensor_tensor(y[1][:, b, 0:H], y[1][:, b, 0:H], 0.0, x_res[:, b, :],
                                                   ALU.max, ALU.add).then_inc(res_done, 1)
                for b in range(QB):
                    wait(dve, res_done, QB * q + b + 1)
                    nc.vector.bn_stats(stat_o[:, b, :], y[1][:, b, 0:H]).then_inc(stats_o_done, 1)
                for b in range(QB):
                    wait_alone(dve, stats_o_done, QB * q + b + 1)
                    last = nc.vector.bn_aggr(mv_o[:, b, :], stat_o[:, b, :])
                last.then_inc(mv_o_done, 1)

            def output_bias(q):
                wait(dve, rstd_o_done, q + 1)
                nc.vector.scalar_tensor_tensor(nb_o[:, :], mv_o[:, :, 0], -1.0, rstd_o[:, :],
                                               ALU.mult, ALU.mult).then_inc(nb_o_done, 1)

            def body(t):
                if has(t):
                    sides_lo(0, t, range(2))
                if has(t - 1):
                    layer_norm(0, t - 1)
                if has(t):
                    sides_lo(0, t, range(2, NG))
                    linear_sum(0, t, range(2))
                if has(t - 1):
                    split_h(1, t - 1)
                if has(t):
                    linear_sum(0, t, range(2, QB))
                    masked_scores(0, t)
                if has(t - 2):
                    layer_stats(1, t - 2)
                if has(t):
                    attention(0, t)
                if has(t - 1):
                    sides_lo(1, t - 1, range(2))
                if has(t - 2):
                    layer_norm(1, t - 2)
                if has(t - 1):
                    sides_lo(1, t - 1, range(2, NG))
                    linear_sum(1, t - 1, range(2))
                if has(t) and has(t + 1):
                    split_h(0, t + 1)
                if has(t - 1):
                    linear_sum(1, t - 1, range(2, QB))
                if has(t - 2):
                    residual(t - 2)
                if has(t - 1):
                    masked_scores(1, t - 1)
                if has(t):
                    layer_stats(0, t)
                if has(t - 1):
                    attention(1, t - 1)
                if has(t - 2):
                    output_bias(t - 2)

            for l in range(L):
                nc.vector.memset(lin_hi[l][:, :, H:H + 1].bitcast(fp32), 1.0)
                nc.vector.memset(lin_hi[l][:, :, H + 1:HX].bitcast(fp32), 0.0)
                last = nc.vector.memset(lin_lo[l][:, :, H:HX].bitcast(fp32), 0.0)
            last.then_inc(pads_done, 1)
            split_h(0, 0)
            for n in range(3 * L):
                l, kind = n // 3, n % 3
                hi, lo = ((w[:, l, kind, :, :] for w in (ws_hi, ws_lo)) if kind < 2 else
                          (w[:, l, :, :] for w in (wl_hi, wl_lo)))
                dve.wait_ge(w_hi_done, n + 1)
                nc.vector.tensor_tensor(lo.rearrange("p c n -> p (c n)"), raw_w[l][kind],
                                        hi.rearrange("p c n -> p (c n)").bitcast(fp32),
                                        ALU.subtract).then_inc(w_lo_done, 1)
            dve.wait_ge(const_done, 1)
            dve.wait_ge(tab_loaded, 16)
            dve.wait_ge(w_lo_done, 3 * L)
            iterations(dve, body)

        @block.gpsimd
        def _(pool):
            def low_part(lo, full, hi):
                return nc.gpsimd.tensor_tensor(lo, full, hi.bitcast(fp32), ALU.subtract)

            def split_h_lo(l, q):
                wait(pool, h_hi_done[l], q + 1)
                low_part(h_lo[l][:, :, :], h32[l][:, :, :], h_hi[l][:, :, :]).then_inc(h_lo_done[l], 1)

            def linear_lo(l, q):
                wait(pool, lin_hi_done[l], q + 1)
                low_part(lin_lo[l][:, :, 0:H], lin32[:, :, :], lin_hi[l][:, :, 0:H]).then_inc(lin_lo_done[l], 1)

            def deviation(l, q):
                wait(pool, mv_done[l], q + 1)
                nc.gpsimd.tensor_tensor(sd[l][:, :], mv[l][:, :, 1], halves[:, 0, :], ALU.pow).then_inc(sd_done[l], 1)

            def make_masks(q):
                wait_alone(pool, adj_loaded, 32 * (q + 1))
                nc.gpsimd.affine_select(out=adj_nat[:, :], in_=adj_nat[:, :], compare_op=ALU.is_gt, fill=0.0,
                                        base=0, pattern=[[0, QB], [1, S]], channel_multiplier=-1).then_inc(mask_step, 1)
                nc.gpsimd.affine_select(out=masks[0][:, 0, :], in_=masks[0][:, 1, :], compare_op=ALU.is_ge, fill=0.0,
                                        base=0, pattern=[[0, QB], [-1, S]], channel_multiplier=1).then_inc(mask_step, 1)
                wait(pool, mask_step, 2 * (q + 1))
                nc.gpsimd.tensor_tensor(masks[0][:, 0, :], masks[0][:, 0, :], adj_nat[:, :],
                                        ALU.add).then_inc(mask_done, 1)

            def affine(q):
                for b in range(QB):
                    wait(pool, z_done[1], QB * q + b + 1)
                    nc.gpsimd.tensor_tensor(y[1][:, b, 0:H], y[1][:, b, 0:H], a_row, ALU.mult).then_inc(aff_mul_done, 1)
                for b in range(QB):
                    wait(pool, aff_mul_done, QB * q + b + 1)
                    nc.gpsimd.tensor_tensor(y[1][:, b, 0:H], y[1][:, b, 0:H], b_row, ALU.add).then_inc(aff_done, 1)

            def output_rstd(q):
                wait_alone(pool, mv_o_done, q + 1)
                nc.gpsimd.tensor_scalar(var_o[:, :], mv_o[:, :, 1], OUT_EPS, None, ALU.add).then_inc(var_o_done, 1)
                wait(pool, var_o_done, q + 1)
                nc.gpsimd.tensor_tensor(rstd_o[:, :], var_o[:, :], halves[:, 1, :], ALU.pow).then_inc(rstd_o_done, 1)

            def body(t):
                if has(t - 1):
                    deviation(0, t - 1)
                if has(t):
                    make_masks(t)
                if has(t - 1):
                    split_h_lo(1, t - 1)
                if has(t):
                    linear_lo(0, t)
                if has(t - 2):
                    deviation(1, t - 2)
                    affine(t - 2)
                if has(t) and has(t + 1):
                    split_h_lo(0, t + 1)
                if has(t - 2):
                    output_rstd(t - 2)
                if has(t - 1):
                    linear_lo(1, t - 1)

            nc.gpsimd.memset(ident[:, :], 0.0).then_inc(const_step, 1)
            nc.gpsimd.memset(use_right[:, :, :], 1).then_inc(const_step, 1)
            nc.gpsimd.memset(halves[:, 0, :], 0.5).then_inc(const_step, 1)
            nc.gpsimd.memset(halves[:, 1, :], -0.5).then_inc(const_step, 1)
            pool.wait_ge(const_step, 4)
            nc.gpsimd.affine_select(out=ident[:, :], in_=ident[:, :], compare_op=ALU.not_equal, fill=1.0, base=0,
                                    pattern=[[-1, P]], channel_multiplier=1).then_inc(const_step, 1)
            nc.gpsimd.affine_select(out=use_right[:, :, :], in_=use_right[:, :, :], compare_op=ALU.is_gt, fill=0.0,
                                    base=0, pattern=[[0, QB], [1, S]], channel_multiplier=-1).then_inc(const_step, 1)
            pool.wait_ge(const_step, 6)
            nc.gpsimd.memset(var_o[:, :], 0.0).then_inc(const_done, 1)
            split_h_lo(0, 0)
            pool.wait_ge(tab_loaded, 16)
            iterations(pool, body)


_OUT = ((128, 128, 384), "float32")


def kernel(**inputs):
    import concourse.bacc as _bacc
    from concourse.bass_utils import run_bass_kernel_spmd as _run

    P, QB = 128, 4
    v = {n: np.asarray(a) for n, a in inputs.items()}
    x, adj = v["x"], v["adj"]
    B, S, H = x.shape
    NQ, HC = B // QB, H // P

    x_t = x.reshape(NQ, QB, S, HC, P).transpose(0, 4, 3, 1, 2).reshape(NQ, P, HC * QB * S)
    a4 = adj.reshape(NQ, QB, S, S)
    adj_pair = np.stack([a4.transpose(0, 2, 1, 3), a4.transpose(0, 3, 1, 2)], axis=2).reshape(NQ, S, 2, QB * S)
    w_side = np.stack([v["L0_gnn_W_left"], v["L0_gnn_W_right"]], axis=1)
    w_lin_t = v["L0_gnn_W_lin"].transpose(0, 2, 1)
    b_lin, ln_a, ln_b = v["L0_gnn_b_lin"], v["L0_gnn_ln_a"], v["L0_gnn_ln_b"]
    rows = np.broadcast_to(np.stack([b_lin[0], b_lin[1], ln_a[1], ln_b[1]])[None], (P, 4, H))
    cols = np.stack([ln_a[0].reshape(HC, P), ln_b[0].reshape(HC, P)]).transpose(2, 0, 1)

    nc = _bacc.Bacc("TRN2", target_bir_lowering=False, num_devices=1)
    arrays, args = {}, []
    for name, a in (("x_nat", x), ("x_t", x_t), ("adj_pair", adj_pair), ("w_side", w_side),
                    ("w_lin_t", w_lin_t), ("rows", rows), ("cols", cols)):
        a = np.ascontiguousarray(a)
        arrays[name] = a
        args.append(nc.dram_tensor(name, a.shape, mybir.dt.from_np(a.dtype), kind="ExternalInput").ap())
    out = nc.dram_tensor("out", _OUT[0], mybir.dt.float32, kind="ExternalOutput").ap()
    gnn_attention_resnorm_kernel(nc, *args, out)
    r = _run(nc, [arrays], core_ids=[0])
    return r.results[0]["out"]
```

```python
import numpy as np
import concourse.bass as bass
from concourse import mybir
from contextlib import ExitStack


def gnn_attention_resnorm_kernel(nc, x_nat, x_t, adj_pair, w_side, w_lin_t, rows, cols, out):
    fp32, fp32r, i32 = mybir.dt.float32, mybir.dt.float32r, mybir.dt.int32
    ALU, ACT = mybir.AluOpType, mybir.ActivationFunctionType

    P = 128
    B, S, H = x_nat.shape
    L = w_lin_t.shape[0]
    QB = 4
    NQ = B // QB
    HC = H // P
    QS = QB * S
    NG = 2 * HC
    GB = 3
    HX = H + 2
    assert S == P and L == 2 and B % QB == 0 and H % P == 0 and QS == 512

    INV_TEMPER = float(1.0 / np.float32(np.sqrt(H)))
    LN_EPS, SUM_EPS, OUT_EPS = 1e-3, 1e-10, 1e-5
    DDOF = float(np.sqrt(H / (H - 1.0)))

    x_q = x_nat.rearrange("(q b) s h -> q s b h", b=QB)
    out_q = out.rearrange("(q b) s h -> q s b h", b=QB)

    FIRST_FULL, END_FULL = 3, NQ - 1
    END = NQ + 2

    ctx = ExitStack()
    with ctx:
        def sb(name, shape, dt=fp32):
            return ctx.enter_context(nc.sbuf_tensor(name, shape, dt))

        def sem(name):
            return ctx.enter_context(nc.semaphore(name))

        def sem_pair(name):
            return [sem(f"{name}{l}") for l in range(L)]

        ws_hi = sb("ws_hi", [P, L, 2, HC, H], fp32r)
        ws_lo = sb("ws_lo", [P, L, 2, HC, H], fp32r)
        wl_hi = sb("wl_hi", [P, L, HC, H], fp32r)
        wl_lo = sb("wl_lo", [P, L, HC, H], fp32r)
        row_tab = sb("row_tab", [P, 4, H])
        b_lin = [row_tab[:, 0, :], row_tab[:, 1, :]]
        a_row, b_row = row_tab[:, 2, :], row_tab[:, 3, :]
        col_tab = sb("col_tab", [P, 2, HC])
        ident = sb("ident", [P, P])
        use_right = sb("use_right", [P, QB, S], i32)
        halves = sb("halves", [P, 2, QB])

        h32 = [sb(f"h32_{l}", [P, HC, QS]) for l in range(L)]
        h_hi = [sb(f"h_hi{l}", [P, HC, QS], fp32r) for l in range(L)]
        h_lo = [sb(f"h_lo{l}", [P, HC, QS], fp32r) for l in range(L)]
        lin_hi = [sb(f"lin_hi{l}", [P, QB, HX], fp32r) for l in range(L)]
        lin_lo = [sb(f"lin_lo{l}", [P, QB, HX], fp32r) for l in range(L)]
        p_hi = [sb(f"p_hi{l}", [P, QS], fp32r) for l in range(L)]
        p_lo = [sb(f"p_lo{l}", [P, QS], fp32r) for l in range(L)]
        y = [sb(f"y{l}", [P, QB, HX]) for l in range(L)]
        masks = [sb(f"masks{l}", [P, 2, QS]) for l in range(L)]
        stat = [sb(f"stat{l}", [P, QB, 6]) for l in range(L)]
        mv = [sb(f"mv{l}", [P, QB, 2]) for l in range(L)]
        sd = [sb(f"sd{l}", [P, QB]) for l in range(L)]
        eps_s = [sb(f"eps_s{l}", [P, QB]) for l in range(L)]
        den = [sb(f"den{l}", [P, QB]) for l in range(L)]
        k_ln = [sb(f"k_ln{l}", [P, QB]) for l in range(L)]
        nb_ln = [sb(f"nb_ln{l}", [P, QB]) for l in range(L)]

        g_hi = sb("g_hi", [P, HC, QB, 2 * S], fp32r)
        g_lo = sb("g_lo", [P, HC, QB, 2 * S], fp32r)
        lin32 = sb("lin32", [P, QB, H])
        score = sb("score", [P, QS])
        p32 = sb("p32", [P, QS])
        adj_nat = sb("adj_nat", [P, QS])
        x_res = sb("x_res", [P, QB, H])
        stat_o = sb("stat_o", [P, QB, 6])
        mv_o = sb("mv_o", [P, QB, 2])
        var_o = sb("var_o", [P, QB])
        rstd_o = sb("rstd_o", [P, QB])
        nb_o = sb("nb_o", [P, QB])
        o_sb = sb("o_sb", [P, QB, H])

        ps_g = ctx.enter_context(nc.psum_tensor("ps_g", [P, GB, QB, S], fp32))
        ps_u = ctx.enter_context(nc.psum_tensor("ps_u", [P, QB, 2 * S], fp32))
        ps_h = ctx.enter_context(nc.psum_tensor("ps_h", [P, 512], fp32))
        ps_c = ctx.enter_context(nc.psum_tensor("ps_c", [P, 2, 512], fp32))

        def lin_bank(b):
            return ps_g[:, 0, :, :].rearrange("p b s -> p (b s)")[:, 0:H] if b % 2 else ps_h[:, 0:H]

        def ctx_bank(b):
            return ps_c[:, (b + 1) % 2, :]

        def stage(t):
            return t[:, :, :].rearrange("p a b -> p (a b)")[:, 0:HC * H]

        raw_w = [[stage(h32[1]), stage(lin32), stage(x_res)], [stage(y[0]), stage(y[1]), stage(o_sb)]]

        w_loaded = [sem(f"w_loaded{n}") for n in range(3 * L)]
        tab_loaded = sem("tab_loaded")
        col_loaded = sem("col_loaded")
        w_hi_done = sem("w_hi_done")
        w_lo_done = sem("w_lo_done")
        const_step = sem("const_step")
        const_done = sem("const_done")
        pads_done = sem("pads_done")
        xt_loaded = sem("xt_loaded")
        adj_loaded = sem("adj_loaded")
        masks_moved = sem("masks_moved")
        xres_loaded = sem("xres_loaded")
        out_stored = sem("out_stored")
        g_done, g_hi_done, g_lo_done = sem_pair("g_done"), sem_pair("g_hi_done"), sem_pair("g_lo_done")
        lin_done, lin_sum_done = sem_pair("lin_done"), sem_pair("lin_sum_done")
        lin_hi_done, lin_lo_done = sem_pair("lin_hi_done"), sem_pair("lin_lo_done")
        u_done, u_sel_done, u_mul_done = sem_pair("u_done"), sem_pair("u_sel_done"), sem_pair("u_mul_done")
        exp_done, p_full_done = sem_pair("exp_done"), sem_pair("p_full_done")
        p_hi_done, p_lo_done = sem_pair("p_hi_done"), sem_pair("p_lo_done")
        ctx_done, y_done = sem_pair("ctx_done"), sem_pair("y_done")
        h_hi_done, h_lo_done = sem_pair("h_hi_done"), sem_pair("h_lo_done")
        stats_done, mv_done, sd_done = sem_pair("stats_done"), sem_pair("mv_done"), sem_pair("sd_done")
        ln_step, z_done = sem_pair("ln_step"), sem_pair("z_done")
        tr_done = sem("tr_done")
        relu_done = sem("relu_done")
        mask_step = sem("mask_step")
        mask_done = sem("mask_done")
        aff_mul_done = sem("aff_mul_done")
        aff_done = sem("aff_done")
        res_done = sem("res_done")
        stats_o_done = sem("stats_o_done")
        mv_o_done = sem("mv_o_done")
        var_o_done = sem("var_o_done")
        rstd_o_done = sem("rstd_o_done")
        nb_o_done = sem("nb_o_done")
        norm_done = sem("norm_done")

        block = ctx.enter_context(nc.Block())

        def wait(eng, s, n):
            if isinstance(n, int) and n <= 0:
                return
            eng.wait_ge(s, n)

        def wait_alone(eng, s, n):
            if not isinstance(n, int):
                eng.compute_val(n)
            eng.wait_ge(const_done, 1)
            wait(eng, s, n)

        def has(q):
            return not isinstance(q, int) or 0 <= q < NQ

        def iterations(eng, body):
            for t in range(FIRST_FULL):
                body(t)
            with eng.Fori(FIRST_FULL, END_FULL) as t:
                body(t)
            for t in range(END_FULL, END):
                body(t)

        def prior(l, q):
            if l == 0:
                return 1, q - 2
            return (0, q + 1) if has(q + 1) else (1, q - 1)

        @block.sync
        def _(sp):
            sp.dma_start(h32[0][:, :, :].rearrange("p c n -> p (c n)"), x_t[0, :, :]).then_inc(xt_loaded, 16)
            for n in range(3 * L):
                l, kind = n // 3, n % 3
                src = w_side[l, kind] if kind < 2 else w_lin_t[l]
                sp.dma_start(raw_w[l][kind].rearrange("p (c n) -> p c n", c=HC),
                             src.rearrange("(c p) n -> p c n", p=P)).then_inc(w_loaded[n], 16)
                if n == 0:
                    sp.dma_start(row_tab[:, :, :], rows).then_inc(tab_loaded, 16)
                    sp.dma_start(col_tab[:, :, :], cols).then_inc(col_loaded, 16)

            def body(t):
                if has(t - 1):
                    wait(sp, p_full_done[1], t - 1)
                    wait(sp, mask_done, t)
                    sp.dma_start(masks[1][:, :, :], masks[0][:, :, :]).then_inc(masks_moved, 16)
                if has(t):
                    wait(sp, masks_moved, 16 * t)
                    wait(sp, p_full_done[0], t)
                    sp.dma_start(masks[0][:, 1, :], adj_pair[t, :, 1, :]).then_inc(adj_loaded, 16)
                    sp.dma_start(adj_nat[:, :], adj_pair[t, :, 0, :]).then_inc(adj_loaded, 16)
                if has(t - 2):
                    wait(sp, res_done, QB * (t - 2))
                    if isinstance(t, int) and t == 2:
                        wait(sp, w_lo_done, 3 * L)
                    sp.dma_start(x_res[:, :, :], x_q[t - 2, :, :, :]).then_inc(xres_loaded, 16)
                if has(t) and has(t + 1):
                    wait(sp, h_hi_done[0], t + 1)
                    wait(sp, h_lo_done[0], t + 1)
                    sp.dma_start(h32[0][:, :, :].rearrange("p c n -> p (c n)"),
                                 x_t[t + 1, :, :]).then_inc(xt_loaded, 16)
                if has(t - 2):
                    wait(sp, norm_done, t - 1)
                    sp.dma_start(out_q[t - 2, :, :, :], o_sb[:, :, :]).then_inc(out_stored, 16)

            iterations(sp, body)
            sp.wait_ge(out_stored, 16 * NQ)

        @block.tensor
        def _(pe):
            def three_passes(out_ap, terms):
                n = len(terms)
                for i, (a_hi, a_lo, b_hi, b_lo) in enumerate(terms):
                    pe.matmul(out_ap, a_hi, b_hi, start=(i == 0), stop=False)
                    pe.matmul(out_ap, a_hi, b_lo, start=False, stop=False)
                    last = pe.matmul(out_ap, a_lo, b_hi, start=False, stop=(i == n - 1))
                return last

            def project_sides(l, q, j):
                if j == 0:
                    wait(pe, h_hi_done[l], q + 1)
                    wait(pe, h_lo_done[l], q + 1)
                    if isinstance(q, int) and q == 0:
                        pe.wait_ge(w_lo_done, 3 * l + 2)
                    pl, pq = prior(l, q)
                    wait(pe, lin_sum_done[pl], QB * (pq + 1))
                if j >= GB:
                    wait(pe, g_lo_done[l], NG * q + j - GB + 1)
                side, m = j % 2, j // 2
                three_passes(ps_g[:, j % GB, :, :].rearrange("p b s -> p (b s)"),
                             [(ws_hi[:, l, side, c, m * P:(m + 1) * P], ws_lo[:, l, side, c, m * P:(m + 1) * P],
                               h_hi[l][:, c, :], h_lo[l][:, c, :]) for c in range(HC)]).then_inc(g_done[l], 1)

            def linear(l, q, b):
                if b == 0:
                    if isinstance(q, int) and q == 0:
                        pe.wait_ge(w_lo_done, 3 * l + 3)
                    pl, pq = prior(l, q)
                    wait(pe, lin_sum_done[pl], QB * pq + 3)
                elif b == 1:
                    wait(pe, g_lo_done[l], NG * q + GB + 1)
                else:
                    wait(pe, lin_sum_done[l], QB * q + b - 1)
                three_passes(lin_bank(b),
                             [(h_hi[l][:, c, b * S:(b + 1) * S], h_lo[l][:, c, b * S:(b + 1) * S],
                               wl_hi[:, l, c, :], wl_lo[:, l, c, :]) for c in range(HC)]).then_inc(lin_done[l], 1)

            def scores(l, q):
                wait(pe, g_lo_done[l], NG * (q + 1))
                pl, pq = prior(l, q)
                wait(pe, u_mul_done[pl], pq + 1)
                for b in range(QB):
                    three_passes(ps_u[:, b, :],
                                 [(h_hi[l][:, c, b * S:(b + 1) * S], h_lo[l][:, c, b * S:(b + 1) * S],
                                   g_hi[:, c, b, :], g_lo[:, c, b, :]) for c in range(HC)]).then_inc(u_done[l], 1)

            def context(l, q, b):
                if b == 0:
                    wait(pe, p_lo_done[l], q + 1)
                    wait(pe, lin_lo_done[l], q + 1)
                if b >= 2:
                    wait(pe, y_done[l], QB * q + b - 1)
                elif l == 1:
                    if has(q + 1):
                        wait(pe, relu_done, HC * (q + 1) + 2 + b)
                    else:
                        wait(pe, y_done[1], QB * (q - 1) + 3 + b)
                else:
                    wait(pe, y_done[1], QB * (q - 2) + 3 + b)
                    if isinstance(q, int) and q == 1:
                        wait(pe, relu_done, HC)
                three_passes(ctx_bank(b)[:, 0:HX],
                             [(p_hi[l][:, b * S:(b + 1) * S], p_lo[l][:, b * S:(b + 1) * S],
                               lin_hi[l][:, b, :], lin_lo[l][:, b, :])]).then_inc(ctx_done[l], 1)

            def transposes(q, c):
                if c == 0:
                    wait(pe, z_done[0], QB * (q + 1))
                if c >= 2:
                    wait(pe, relu_done, HC * q + c - 1)
                for b in range(QB):
                    last = pe.transpose(ps_c[:, c % 2, b * S:(b + 1) * S], y[0][:, b, c * P:(c + 1) * P],
                                        ident[:, :])
                last.then_inc(tr_done, 1)

            def body(t):
                for j in range(NG):
                    if has(t):
                        project_sides(0, t, j)
                    if has(t - 1) and 1 <= j <= HC:
                        transposes(t - 1, j - 1)
                for b in range(QB):
                    if has(t):
                        linear(0, t, b)
                    if has(t - 2):
                        context(1, t - 2, b)
                if has(t):
                    scores(0, t)
                if has(t - 1):
                    for j in range(NG):
                        project_sides(1, t - 1, j)
                for b in range(QB):
                    if has(t - 1):
                        linear(1, t - 1, b)
                    if has(t):
                        context(0, t, b)
                if has(t - 1):
                    scores(1, t - 1)

            pe.wait_ge(const_done, 1)
            pe.wait_ge(pads_done, 1)
            iterations(pe, body)

        @block.scalar
        def _(act):
            for n in range(3 * L):
                l, kind = n // 3, n % 3
                act.wait_ge(w_loaded[n], 16)
                dst = ws_hi[:, l, kind, :, :] if kind < 2 else wl_hi[:, l, :, :]
                nc.scalar.activation(dst.rearrange("p c n -> p (c n)"), raw_w[l][kind], ACT.Copy).then_inc(w_hi_done, 1)
            act.wait_ge(col_loaded, 16)

            def sides_hi(l, q, j):
                side, m = j % 2, j // 2
                if j == 0:
                    pl, pq = prior(l, q)
                    wait(act, u_done[pl], QB * (pq + 1))
                wait(act, g_done[l], NG * q + j + 1)
                nc.scalar.activation(g_hi[:, m, :, side * S:(side + 1) * S], ps_g[:, j % GB, :, :],
                                     ACT.Copy).then_inc(g_hi_done[l], 1)

            def relu_affine(q, c):
                if c == 0:
                    wait(act, h_hi_done[1], q)
                    wait(act, h_lo_done[1], q)
                    if isinstance(q, int) and q == 0:
                        act.wait_ge(w_lo_done, 3 * L)
                wait(act, tr_done, HC * q + c + 1)
                nc.scalar.activation(h32[1][:, c, :], ps_c[:, c % 2, :], ACT.Relu, bias=col_tab[:, 1, c:c + 1],
                                     scale=col_tab[:, 0, c:c + 1]).then_inc(relu_done, 1)

            def linear_hi(l, q):
                wait(act, lin_sum_done[l], QB * (q + 1))
                wait(act, ctx_done[l], QB * q)
                nc.scalar.activation(lin_hi[l][:, :, 0:H], lin32[:, :, :], ACT.Copy).then_inc(lin_hi_done[l], 1)

            def take_context(l, q, b):
                if b == 0:
                    if l == 0:
                        wait(act, tr_done, HC * q)
                    else:
                        wait(act, norm_done, q)
                    if isinstance(q, int) and q == 0:
                        act.wait_ge(w_lo_done, 3 * L)
                wait(act, ctx_done[l], QB * q + b + 1)
                nc.scalar.activation(y[l][:, b, 0:H + 1], ctx_bank(b)[:, 0:H + 1], ACT.Copy).then_inc(y_done[l], 1)

            def exponentials(l, q):
                wait(act, u_mul_done[l], q + 1)
                nc.scalar.activation(score[:, :], score[:, :], ACT.Exp, scale=INV_TEMPER).then_inc(exp_done[l], 1)

            def output_norm(q):
                wait(act, nb_o_done, q + 1)
                wait(act, out_stored, 16 * q)
                for b in range(QB):
                    last = nc.scalar.activation(o_sb[:, b, :], y[1][:, b, 0:H], ACT.Identity,
                                                bias=nb_o[:, b:b + 1], scale=rstd_o[:, b:b + 1])
                last.then_inc(norm_done, 1)

            def body(t):
                if has(t - 2):
                    exponentials(1, t - 2)
                for j in range(NG):
                    if has(t):
                        sides_hi(0, t, j)
                    if has(t - 1) and 1 <= j <= HC:
                        relu_affine(t - 1, j - 1)
                for b in range(QB):
                    if b == QB - 1 and has(t):
                        linear_hi(0, t)
                    if has(t - 2):
                        take_context(1, t - 2, b)
                if has(t):
                    exponentials(0, t)
                if has(t - 1):
                    for j in range(NG):
                        sides_hi(1, t - 1, j)
                for b in range(QB):
                    if b == QB - 1 and has(t - 1):
                        linear_hi(1, t - 1)
                    if has(t):
                        take_context(0, t, b)
                if has(t - 2):
                    output_norm(t - 2)

            iterations(act, body)

        @block.vector
        def _(dve):
            def split_h(l, q):
                if l == 0:
                    wait(dve, xt_loaded, 16 * (q + 1))
                else:
                    wait(dve, relu_done, HC * (q + 1))
                wait(dve, u_done[l], QB * q)
                nc.vector.tensor_copy(h_hi[l][:, :, :], h32[l][:, :, :]).then_inc(h_hi_done[l], 1)

            def sides_lo(l, q, j):
                side, m = j % 2, j // 2
                wait(dve, g_hi_done[l], NG * q + j + 1)
                cols_j = slice(side * S, (side + 1) * S)
                nc.vector.tensor_tensor(g_lo[:, m, :, cols_j], ps_g[:, j % GB, :, :],
                                        g_hi[:, m, :, cols_j].bitcast(fp32), ALU.subtract).then_inc(g_lo_done[l], 1)

            def linear_sum(l, q, b):
                if b == 0:
                    pl, pq = prior(l, q)
                    wait(dve, lin_hi_done[pl], pq + 1)
                    wait(dve, lin_lo_done[pl], pq + 1)
                wait(dve, lin_done[l], QB * q + b + 1)
                nc.vector.tensor_tensor(lin32[:, b, :], lin_bank(b), b_lin[l], ALU.add).then_inc(lin_sum_done[l], 1)

            def masked_scores(l, q):
                wait_alone(dve, u_done[l], QB * (q + 1))
                nc.vector.copy_predicated(ps_u[:, :, 0:S], use_right[:, :, :],
                                          ps_u[:, :, S:2 * S]).then_inc(u_sel_done[l], 1)
                wait(dve, u_sel_done[l], q + 1)
                if l == 0:
                    wait(dve, mask_done, q + 1)
                else:
                    wait(dve, masks_moved, 16 * (q + 1))
                nc.vector.tensor_tensor(score[:, :].rearrange("p (b s) -> p b s", b=QB), ps_u[:, :, 0:S],
                                        masks[l][:, 0, :].rearrange("p (b s) -> p b s", b=QB),
                                        ALU.mult).then_inc(u_mul_done[l], 1)

            def attention_hi(l, q):
                wait(dve, exp_done[l], q + 1)
                nc.vector.tensor_tensor(p32[:, :], score[:, :], masks[l][:, 1, :], ALU.mult).then_inc(p_full_done[l], 1)
                wait(dve, p_full_done[l], q + 1)
                wait(dve, ctx_done[l], QB * q)
                nc.vector.tensor_copy(p_hi[l][:, :], p32[:, :]).then_inc(p_hi_done[l], 1)

            def attention_lo(l, q):
                wait(dve, p_hi_done[l], q + 1)
                nc.vector.tensor_tensor(p_lo[l][:, :], p32[:, :], p_hi[l][:, :].bitcast(fp32),
                                        ALU.subtract).then_inc(p_lo_done[l], 1)

            def layer_stats(l, q, b):
                wait(dve, y_done[l], QB * q + b + 1)
                nc.vector.bn_stats(stat[l][:, b, :], y[l][:, b, 0:H]).then_inc(stats_done[l], 1)

            def layer_moments(l, q):
                for b in range(QB):
                    wait_alone(dve, stats_done[l], QB * q + b + 1)
                    last = nc.vector.bn_aggr(mv[l][:, b, :], stat[l][:, b, :])
                last.then_inc(mv_done[l], 1)
                nc.vector.tensor_scalar(eps_s[l][:, :], y[l][:, :, H], LN_EPS, LN_EPS * SUM_EPS,
                                        ALU.mult, ALU.add).then_inc(ln_step[l], 1)

            def layer_norm(l, q):
                wait(dve, sd_done[l], q + 1)
                wait(dve, ln_step[l], 4 * q + 1)
                nc.vector.scalar_tensor_tensor(den[l][:, :], sd[l][:, :], DDOF, eps_s[l][:, :],
                                               ALU.mult, ALU.add).then_inc(ln_step[l], 1)
                wait(dve, ln_step[l], 4 * q + 2)
                nc.vector.reciprocal(k_ln[l][:, :], den[l][:, :]).then_inc(ln_step[l], 1)
                wait(dve, ln_step[l], 4 * q + 3)
                nc.vector.scalar_tensor_tensor(nb_ln[l][:, :], mv[l][:, :, 0], -1.0, k_ln[l][:, :],
                                               ALU.mult, ALU.mult).then_inc(ln_step[l], 1)
                wait(dve, ln_step[l], 4 * q + 4)
                for b in range(QB):
                    nc.vector.tensor_scalar(y[l][:, b, 0:H], y[l][:, b, 0:H], k_ln[l][:, b:b + 1],
                                            nb_ln[l][:, b:b + 1], ALU.mult, ALU.add).then_inc(z_done[l], 1)

            def residual(q, b):
                if b == 0:
                    wait(dve, xres_loaded, 16 * (q + 1))
                wait(dve, aff_done, QB * q + b + 1)
                nc.vector.scalar_tensor_tensor(y[1][:, b, 0:H], y[1][:, b, 0:H], 0.0, x_res[:, b, :],
                                               ALU.max, ALU.add).then_inc(res_done, 1)

            def output_stats(q, b):
                wait(dve, res_done, QB * q + b + 1)
                nc.vector.bn_stats(stat_o[:, b, :], y[1][:, b, 0:H]).then_inc(stats_o_done, 1)

            def output_moments(q):
                for b in range(QB):
                    wait_alone(dve, stats_o_done, QB * q + b + 1)
                    last = nc.vector.bn_aggr(mv_o[:, b, :], stat_o[:, b, :])
                last.then_inc(mv_o_done, 1)

            def output_bias(q):
                wait(dve, rstd_o_done, q + 1)
                nc.vector.scalar_tensor_tensor(nb_o[:, :], mv_o[:, :, 0], -1.0, rstd_o[:, :],
                                               ALU.mult, ALU.mult).then_inc(nb_o_done, 1)

            def body(t):
                if has(t - 2):
                    masked_scores(1, t - 2)
                for j in range(NG):
                    if has(t):
                        sides_lo(0, t, j)
                    if has(t - 2) and j == 0:
                        attention_hi(1, t - 2)
                    if has(t - 2) and j == 1:
                        attention_lo(1, t - 2)
                    if has(t - 1) and j == HC + 1:
                        split_h(1, t - 1)
                for b in range(QB + 1):
                    if has(t) and b < QB:
                        linear_sum(0, t, b)
                    if has(t - 2) and b > 0:
                        layer_stats(1, t - 2, b - 1)
                if has(t - 2):
                    layer_moments(1, t - 2)
                    layer_norm(1, t - 2)
                if has(t):
                    masked_scores(0, t)
                for j in range(NG):
                    if has(t - 1):
                        sides_lo(1, t - 1, j)
                    if has(t) and j == 0:
                        attention_hi(0, t)
                    if has(t) and j == 1:
                        attention_lo(0, t)
                    if has(t) and has(t + 1) and j == 2:
                        split_h(0, t + 1)
                    if has(t - 2) and j >= 4:
                        residual(t - 2, 2 * (j - 4))
                        residual(t - 2, 2 * (j - 4) + 1)
                for b in range(QB + 1):
                    if has(t - 1) and b < QB:
                        linear_sum(1, t - 1, b)
                    if has(t) and b > 0:
                        layer_stats(0, t, b - 1)
                    if has(t - 2) and b > 0:
                        output_stats(t - 2, b - 1)
                if has(t):
                    layer_moments(0, t)
                if has(t - 2):
                    output_moments(t - 2)
                if has(t):
                    layer_norm(0, t)
                if has(t - 2):
                    output_bias(t - 2)

            for l in range(L):
                nc.vector.memset(lin_hi[l][:, :, H:H + 1].bitcast(fp32), 1.0)
                nc.vector.memset(lin_hi[l][:, :, H + 1:HX].bitcast(fp32), 0.0)
                last = nc.vector.memset(lin_lo[l][:, :, H:HX].bitcast(fp32), 0.0)
            last.then_inc(pads_done, 1)
            split_h(0, 0)
            for n in range(3 * L):
                l, kind = n // 3, n % 3
                hi, lo = ((w[:, l, kind, :, :] for w in (ws_hi, ws_lo)) if kind < 2 else
                          (w[:, l, :, :] for w in (wl_hi, wl_lo)))
                dve.wait_ge(w_hi_done, n + 1)
                nc.vector.tensor_tensor(lo.rearrange("p c n -> p (c n)"), raw_w[l][kind],
                                        hi.rearrange("p c n -> p (c n)").bitcast(fp32),
                                        ALU.subtract).then_inc(w_lo_done, 1)
            dve.wait_ge(const_done, 1)
            dve.wait_ge(tab_loaded, 16)
            dve.wait_ge(w_lo_done, 3 * L)
            iterations(dve, body)

        @block.gpsimd
        def _(pool):
            def low_part(lo, full, hi):
                return nc.gpsimd.tensor_tensor(lo, full, hi.bitcast(fp32), ALU.subtract)

            def split_h_lo(l, q):
                wait(pool, h_hi_done[l], q + 1)
                low_part(h_lo[l][:, :, :], h32[l][:, :, :], h_hi[l][:, :, :]).then_inc(h_lo_done[l], 1)

            def linear_lo(l, q):
                wait(pool, lin_hi_done[l], q + 1)
                low_part(lin_lo[l][:, :, 0:H], lin32[:, :, :], lin_hi[l][:, :, 0:H]).then_inc(lin_lo_done[l], 1)

            def deviation(l, q):
                wait(pool, mv_done[l], q + 1)
                nc.gpsimd.tensor_tensor(sd[l][:, :], mv[l][:, :, 1], halves[:, 0, :], ALU.pow).then_inc(sd_done[l], 1)

            def make_masks(q):
                wait_alone(pool, adj_loaded, 32 * (q + 1))
                nc.gpsimd.affine_select(out=adj_nat[:, :], in_=adj_nat[:, :], compare_op=ALU.is_gt, fill=0.0,
                                        base=0, pattern=[[0, QB], [1, S]], channel_multiplier=-1).then_inc(mask_step, 1)
                nc.gpsimd.affine_select(out=masks[0][:, 0, :], in_=masks[0][:, 1, :], compare_op=ALU.is_ge, fill=0.0,
                                        base=0, pattern=[[0, QB], [-1, S]], channel_multiplier=1).then_inc(mask_step, 1)
                wait(pool, mask_step, 2 * (q + 1))
                nc.gpsimd.tensor_tensor(masks[0][:, 0, :], masks[0][:, 0, :], adj_nat[:, :],
                                        ALU.add).then_inc(mask_done, 1)

            def affine(q):
                for n in range(QB + 1):
                    if n < QB:
                        wait(pool, z_done[1], QB * q + n + 1)
                        nc.gpsimd.tensor_tensor(y[1][:, n, 0:H], y[1][:, n, 0:H], a_row,
                                                ALU.mult).then_inc(aff_mul_done, 1)
                    if n > 0:
                        wait(pool, aff_mul_done, QB * q + n)
                        nc.gpsimd.tensor_tensor(y[1][:, n - 1, 0:H], y[1][:, n - 1, 0:H], b_row,
                                                ALU.add).then_inc(aff_done, 1)

            def output_rstd(q):
                wait_alone(pool, mv_o_done, q + 1)
                nc.gpsimd.tensor_scalar(var_o[:, :], mv_o[:, :, 1], OUT_EPS, None, ALU.add).then_inc(var_o_done, 1)
                wait(pool, var_o_done, q + 1)
                nc.gpsimd.tensor_tensor(rstd_o[:, :], var_o[:, :], halves[:, 1, :], ALU.pow).then_inc(rstd_o_done, 1)

            def body(t):
                if has(t - 1):
                    split_h_lo(1, t - 1)
                if has(t):
                    make_masks(t)
                if has(t - 2):
                    deviation(1, t - 2)
                if has(t):
                    linear_lo(0, t)
                if has(t - 2):
                    affine(t - 2)
                if has(t) and has(t + 1):
                    split_h_lo(0, t + 1)
                if has(t):
                    deviation(0, t)
                if has(t - 2):
                    output_rstd(t - 2)
                if has(t - 1):
                    linear_lo(1, t - 1)

            nc.gpsimd.memset(ident[:, :], 0.0).then_inc(const_step, 1)
            nc.gpsimd.memset(use_right[:, :, :], 1).then_inc(const_step, 1)
            nc.gpsimd.memset(halves[:, 0, :], 0.5).then_inc(const_step, 1)
            nc.gpsimd.memset(halves[:, 1, :], -0.5).then_inc(const_step, 1)
            pool.wait_ge(const_step, 4)
            nc.gpsimd.affine_select(out=ident[:, :], in_=ident[:, :], compare_op=ALU.not_equal, fill=1.0, base=0,
                                    pattern=[[-1, P]], channel_multiplier=1).then_inc(const_step, 1)
            nc.gpsimd.affine_select(out=use_right[:, :, :], in_=use_right[:, :, :], compare_op=ALU.is_gt, fill=0.0,
                                    base=0, pattern=[[0, QB], [1, S]], channel_multiplier=-1).then_inc(const_step, 1)
            pool.wait_ge(const_step, 6)
            nc.gpsimd.memset(var_o[:, :], 0.0).then_inc(const_done, 1)
            split_h_lo(0, 0)
            pool.wait_ge(tab_loaded, 16)
            iterations(pool, body)


_OUT = ((128, 128, 384), "float32")


def kernel(**inputs):
    import concourse.bacc as _bacc
    from concourse.bass_utils import run_bass_kernel_spmd as _run

    P, QB = 128, 4
    v = {n: np.asarray(a) for n, a in inputs.items()}
    x, adj = v["x"], v["adj"]
    B, S, H = x.shape
    NQ, HC = B // QB, H // P

    x_t = x.reshape(NQ, QB, S, HC, P).transpose(0, 4, 3, 1, 2).reshape(NQ, P, HC * QB * S)
    a4 = adj.reshape(NQ, QB, S, S)
    adj_pair = np.stack([a4.transpose(0, 2, 1, 3), a4.transpose(0, 3, 1, 2)], axis=2).reshape(NQ, S, 2, QB * S)
    w_side = np.stack([v["L0_gnn_W_left"], v["L0_gnn_W_right"]], axis=1)
    w_lin_t = v["L0_gnn_W_lin"].transpose(0, 2, 1)
    b_lin, ln_a, ln_b = v["L0_gnn_b_lin"], v["L0_gnn_ln_a"], v["L0_gnn_ln_b"]
    rows = np.broadcast_to(np.stack([b_lin[0], b_lin[1], ln_a[1], ln_b[1]])[None], (P, 4, H))
    cols = np.stack([ln_a[0].reshape(HC, P), ln_b[0].reshape(HC, P)]).transpose(2, 0, 1)

    nc = _bacc.Bacc("TRN2", target_bir_lowering=False, num_devices=1)
    arrays, args = {}, []
    for name, a in (("x_nat", x), ("x_t", x_t), ("adj_pair", adj_pair), ("w_side", w_side),
                    ("w_lin_t", w_lin_t), ("rows", rows), ("cols", cols)):
        a = np.ascontiguousarray(a)
        arrays[name] = a
        args.append(nc.dram_tensor(name, a.shape, mybir.dt.from_np(a.dtype), kind="ExternalInput").ap())
    out = nc.dram_tensor("out", _OUT[0], mybir.dt.float32, kind="ExternalOutput").ap()
    gnn_attention_resnorm_kernel(nc, *args, out)
    r = _run(nc, [arrays], core_ids=[0])
    return r.results[0]["out"]
```

```python
import numpy as np
import concourse.bass as bass
from concourse import mybir
from contextlib import ExitStack


def gnn_attention_resnorm_kernel(nc, x_nat, x_t, adj_pair, w_side, w_lin_t, rows, cols, out):
    fp32, fp32r, i32 = mybir.dt.float32, mybir.dt.float32r, mybir.dt.int32
    ALU, ACT = mybir.AluOpType, mybir.ActivationFunctionType

    P = 128
    B, S, H = x_nat.shape
    L = w_lin_t.shape[0]
    QB = 4
    NQ = B // QB
    HC = H // P
    QS = QB * S
    NG = 2 * HC
    GB = 3
    BW = 32
    NB = P // BW
    HX = H + 2
    assert S == P and L == 2 and B % QB == 0 and H % P == 0 and QS == 512

    INV_TEMPER = float(1.0 / np.float32(np.sqrt(H)))
    LN_EPS, SUM_EPS, OUT_EPS = 1e-3, 1e-10, 1e-5
    DDOF = float(np.sqrt(H / (H - 1.0)))

    x_q = x_nat.rearrange("(q b) s h -> q s b h", b=QB)
    out_q = out.rearrange("(q b) s h -> q s b h", b=QB)

    FIRST_FULL, END_FULL = 3, NQ - 1
    END = NQ + 2

    ctx = ExitStack()
    with ctx:
        def sb(name, shape, dt=fp32):
            return ctx.enter_context(nc.sbuf_tensor(name, shape, dt))

        def sem(name):
            return ctx.enter_context(nc.semaphore(name))

        def sem_pair(name):
            return [sem(f"{name}{l}") for l in range(L)]

        ws_hi = sb("ws_hi", [P, L, 2, HC, H], fp32r)
        ws_lo = sb("ws_lo", [P, L, 2, HC, H], fp32r)
        wl_hi = sb("wl_hi", [P, L, HC, H], fp32r)
        wl_lo = sb("wl_lo", [P, L, HC, H], fp32r)
        row_tab = sb("row_tab", [P, 4, H])
        b_lin = [row_tab[:, 0, :], row_tab[:, 1, :]]
        a_row, b_row = row_tab[:, 2, :], row_tab[:, 3, :]
        col_tab = sb("col_tab", [P, 2, HC])
        ident = sb("ident", [P, P])
        use_right = sb("use_right", [P, QB, S], i32)
        halves = sb("halves", [P, 2, QB])

        h32 = [sb(f"h32_{l}", [P, HC, QS]) for l in range(L)]
        h_hi = [sb(f"h_hi{l}", [P, HC, QS], fp32r) for l in range(L)]
        h_lo = [sb(f"h_lo{l}", [P, HC, QS], fp32r) for l in range(L)]
        lin_hi = [sb(f"lin_hi{l}", [P, QB, HX], fp32r) for l in range(L)]
        lin_lo = [sb(f"lin_lo{l}", [P, QB, HX], fp32r) for l in range(L)]
        p_hi = [sb(f"p_hi{l}", [P, QS], fp32r) for l in range(L)]
        p_lo = [sb(f"p_lo{l}", [P, QS], fp32r) for l in range(L)]
        y = [sb(f"y{l}", [P, QB, HX]) for l in range(L)]
        masks = [sb(f"masks{l}", [P, 2, QS]) for l in range(L)]
        stat = [sb(f"stat{l}", [P, QB, 6]) for l in range(L)]
        mv = [sb(f"mv{l}", [P, QB, 2]) for l in range(L)]
        sd = [sb(f"sd{l}", [P, QB]) for l in range(L)]
        eps_s = [sb(f"eps_s{l}", [P, QB]) for l in range(L)]
        den = [sb(f"den{l}", [P, QB]) for l in range(L)]
        k_ln = [sb(f"k_ln{l}", [P, QB]) for l in range(L)]
        nb_ln = sb("nb_ln", [P, QB])

        z_t = sb("z_t", [P, NB, HC, QB, BW])
        g_hi = sb("g_hi", [P, HC, QB, 2 * S], fp32r)
        g_lo = sb("g_lo", [P, HC, QB, 2 * S], fp32r)
        lin32 = sb("lin32", [P, QB, H])
        score = sb("score", [P, QS])
        p32 = sb("p32", [P, QS])
        adj_nat = sb("adj_nat", [P, QS])
        x_res = sb("x_res", [P, QB, H])
        stat_o = sb("stat_o", [P, QB, 6])
        mv_o = sb("mv_o", [P, QB, 2])
        var_o = sb("var_o", [P, QB])
        rstd_o = sb("rstd_o", [P, QB])
        nb_o = sb("nb_o", [P, QB])
        o_sb = sb("o_sb", [P, QB, H])

        ps_g = ctx.enter_context(nc.psum_tensor("ps_g", [P, GB, QB, S], fp32))
        ps_u = ctx.enter_context(nc.psum_tensor("ps_u", [P, QB, 2 * S], fp32))
        ps_h = ctx.enter_context(nc.psum_tensor("ps_h", [P, 512], fp32))
        ps_c = ctx.enter_context(nc.psum_tensor("ps_c", [P, 2, 512], fp32))

        def lin_bank(b):
            return ps_g[:, 0, :, :].rearrange("p b s -> p (b s)")[:, 0:H] if b % 2 else ps_h[:, 0:H]

        def ctx_bank(b):
            return ps_c[:, b % 2, :]

        h32_blocks = h32[1][:, :, :].rearrange("p c n -> p (c n)").rearrange(
            "p (a c b i) -> p a c b i", a=NB, c=HC, b=QB)

        def h32_chunk(l, c):
            return h32_blocks[:, :, c, :, :].rearrange("p a b i -> p b a i") if l == 1 else h32[0][:, c, :]

        def split_chunk(h_part, l, c):
            flat = h_part[:, c, :]
            return flat.rearrange("p (b a i) -> p b a i", b=QB, a=NB) if l == 1 else flat

        def stage(t):
            return t[:, :, :].rearrange("p a b -> p (a b)")[:, 0:HC * H]

        def at(t, n):
            return isinstance(t, int) and t == n

        def own_set(l, q):
            return 0 if at(q, NQ - 1) else l

        def is_edge(l, q):
            return isinstance(q, int) and (l, q) in ((0, 0), (0, 1), (1, 0), (1, NQ - 1))

        def residual_buffer(q):
            if at(q, NQ - 1):
                return h32[0][:, :, :].rearrange("p c n -> p (c n)").rearrange("p (b h) -> p b h", b=QB)
            return x_res[:, :, :]

        W0_STEPS = HC

        def weight_steps(n):
            return W0_STEPS + n

        raw_w = [[stage(h32[1]), stage(lin32), stage(x_res)], [stage(y[0]), stage(y[1]), stage(o_sb)]]

        x0_loaded = [sem(f"x0_loaded{c}") for c in range(HC)]
        w0_loaded = [sem(f"w0_loaded{c}") for c in range(HC)]
        w_loaded = {n: sem(f"w_loaded{n}") for n in range(1, 3 * L)}
        tab_loaded = sem("tab_loaded")
        col_loaded = sem("col_loaded")
        w_hi_done = sem("w_hi_done")
        w_lo_done = sem("w_lo_done")
        const_step = sem("const_step")
        const_done = sem("const_done")
        pads_done = sem("pads_done")
        xt_loaded = sem("xt_loaded")
        adj_loaded = sem("adj_loaded")
        masks_moved = sem("masks_moved")
        xres_loaded = sem("xres_loaded")
        out_stored = sem("out_stored")
        g_done, g_hi_done, g_lo_done = sem_pair("g_done"), sem_pair("g_hi_done"), sem_pair("g_lo_done")
        lin_done, lin_sum_done = sem_pair("lin_done"), sem_pair("lin_sum_done")
        lin_hi_done, lin_lo_done = sem_pair("lin_hi_done"), sem_pair("lin_lo_done")
        u_done, u_sel_done, u_mul_done = sem_pair("u_done"), sem_pair("u_sel_done"), sem_pair("u_mul_done")
        exp_done, p_full_done = sem_pair("exp_done"), sem_pair("p_full_done")
        p_hi_done, p_lo_done = sem_pair("p_hi_done"), sem_pair("p_lo_done")
        ctx_done, y_done = sem_pair("ctx_done"), sem_pair("y_done")
        h_hi_done, h_lo_done = sem_pair("h_hi_done"), sem_pair("h_lo_done")
        stats_done, mv_done, sd_done = sem_pair("stats_done"), sem_pair("mv_done"), sem_pair("sd_done")
        eps_done, den_done, k_done = sem_pair("eps_done"), sem_pair("den_done"), sem_pair("k_done")
        nb_done = sem("nb_done")
        z_done = sem("z_done")
        tr_done = sem("tr_done")
        turned = sem("turned")
        z_moved = sem("z_moved")
        relu_done = sem("relu_done")
        mask_step = sem("mask_step")
        mask_done = sem("mask_done")
        scale_a_done = sem("scale_a_done")
        affine_done = sem("affine_done")
        res_done = sem("res_done")
        stats_o_done = sem("stats_o_done")
        mv_o_done = sem("mv_o_done")
        var_o_done = sem("var_o_done")
        rstd_o_done = sem("rstd_o_done")
        nb_o_done = sem("nb_o_done")
        norm_done = sem("norm_done")
        last_half_done = sem("last_half_done")

        LAST_BUT_ONE = [[], [], [0, 1], [2], [3], []]

        block = ctx.enter_context(nc.Block())

        def wait(eng, s, n):
            if isinstance(n, int) and n <= 0:
                return
            eng.wait_ge(s, n)

        def wait_alone(eng, s, n):
            if not isinstance(n, int):
                eng.compute_val(n)
            eng.wait_ge(const_done, 1)
            wait(eng, s, n)

        def has(q):
            return not isinstance(q, int) or 0 <= q < NQ

        def iterations(eng, body):
            for t in range(FIRST_FULL):
                body(t)
            with eng.Fori(FIRST_FULL, END_FULL) as t:
                body(t)
            for t in range(END_FULL, END):
                body(t)

        def prior(l, q):
            if l == 0:
                return (1, q - 2) if has(q - 2) else (0, q - 1)
            return (0, q + 1) if has(q + 1) else (1, q - 1)

        def by_tensor(q):
            return at(q, 0) or at(q, NQ - 1)

        def tr_count(q):
            return HC if at(q, 0) else 2 * HC

        def is_end(l, q):
            return isinstance(q, int) and (l, q) in ((0, 0), (1, NQ - 1))

        @block.sync
        def _(sp):
            def load_masks(t):
                sp.dma_start(masks[0][:, 1, :], adj_pair[t, :, 1, :]).then_inc(adj_loaded, 16)
                sp.dma_start(adj_nat[:, :], adj_pair[t, :, 0, :]).then_inc(adj_loaded, 16)

            for c in range(HC):
                sp.dma_start(h32[0][:, c, :], x_t[0, :, c * QS:(c + 1) * QS]).then_inc(x0_loaded[c], 16)
                sp.dma_start(raw_w[0][0][:, c * H:(c + 1) * H],
                             w_side[0, 0, c * P:(c + 1) * P, :]).then_inc(w0_loaded[c], 16)
            for n in range(1, 3 * L):
                l, kind = n // 3, n % 3
                src = w_side[l, kind] if kind < 2 else w_lin_t[l]
                sp.dma_start(raw_w[l][kind].rearrange("p (c n) -> p c n", c=HC),
                             src.rearrange("(c p) n -> p c n", p=P)).then_inc(w_loaded[n], 16)
                if n == 2:
                    load_masks(0)
                    sp.dma_start(row_tab[:, :, :], rows).then_inc(tab_loaded, 16)
                    sp.dma_start(col_tab[:, :, :], cols).then_inc(col_loaded, 16)

            def body(t):
                if has(t - 1):
                    wait(sp, p_full_done[1], t - 1)
                    wait(sp, mask_done, t)
                    sp.dma_start(masks[1][:, :, :], masks[0][:, :, :]).then_inc(masks_moved, 16)
                if has(t) and has(t - 1):
                    wait(sp, masks_moved, 16 * t)
                    wait(sp, p_full_done[0], t)
                    load_masks(t)
                if has(t - 2) and not at(t, NQ + 1):
                    wait(sp, res_done, QB * (t - 2))
                    if at(t, 2):
                        wait(sp, w_lo_done, weight_steps(3 * L - 1))
                    sp.dma_start(x_res[:, :, :], x_q[t - 2, :, :, :]).then_inc(xres_loaded, 16)
                if at(t, NQ):
                    wait(sp, h_lo_done[0], HC * NQ)
                    wait(sp, xres_loaded, 16 * (NQ - 1))
                    sp.dma_start(residual_buffer(NQ - 1), x_q[NQ - 1, :, :, :]).then_inc(xres_loaded, 16)
                if has(t) and has(t + 1):
                    wait(sp, h_hi_done[0], HC * (t + 1))
                    wait(sp, h_lo_done[0], HC * (t + 1))
                    sp.dma_start(h32[0][:, :, :].rearrange("p c n -> p (c n)"),
                                 x_t[t + 1, :, :]).then_inc(xt_loaded, 16)
                if has(t - 2) and not at(t, NQ + 1):
                    wait(sp, norm_done, t - 1)
                    sp.dma_start(out_q[t - 2, :, :, :], o_sb[:, :, :]).then_inc(out_stored, 16)
                elif at(t, NQ + 1):
                    for half, done in ((slice(0, QB // 2), (norm_done, NQ)), (slice(QB // 2, QB), (last_half_done, 1))):
                        sp.wait_ge(*done)
                        sp.dma_start(out_q[NQ - 1, :, half, :], o_sb[:, half, :]).then_inc(out_stored, 16)
                if has(t) and not by_tensor(t):
                    if not isinstance(t, int):
                        sp.compute_val(HC * t)
                    wait(sp, turned, QB * t)
                    wait(sp, h_hi_done[1], HC * t)
                    wait(sp, h_lo_done[1], HC * t)
                    for a in range(NB):
                        for f in range(NB):
                            sp.dma_start(h32_blocks[BW * f:BW * (f + 1), a, :, :, :],
                                         z_t[BW * a:BW * (a + 1), f, :, :, :]).then_inc(z_moved, 16)

            iterations(sp, body)
            sp.wait_ge(out_stored, 16 * (NQ + 1))

        @block.tensor
        def _(pe):
            def three_passes(out_ap, a_hi, a_lo, b_hi, b_lo, first=True, last=True):
                pe.matmul(out_ap, a_hi, b_hi, start=first, stop=False)
                pe.matmul(out_ap, a_hi, b_lo, start=False, stop=False)
                return pe.matmul(out_ap, a_lo, b_hi, start=False, stop=last)

            def project_sides(l, q, j):
                n = own_set(l, q)
                side, m = j // HC, j % HC
                if j == 0:
                    if not is_edge(l, q):
                        wait(pe, h_hi_done[l], HC * (q + 1))
                        wait(pe, h_lo_done[l], HC * (q + 1))
                    pl, pq = prior(l, q)
                    wait(pe, lin_sum_done[pl], QB * (pq + 1))
                if j >= GB:
                    wait(pe, g_lo_done[l], NG * q + j - GB + 1)
                if at(q, 0) and m == 0 and (l, side) != (0, 0):
                    pe.wait_ge(w_lo_done, weight_steps(3 * l + side))
                for c in range(HC):
                    if j == 0 and is_edge(l, q):
                        wait(pe, h_hi_done[l], HC * q + c + 1)
                        wait(pe, h_lo_done[l], HC * q + c + 1)
                        if l == 0 and at(q, 0):
                            pe.wait_ge(w_lo_done, c + 1)
                    last = three_passes(ps_g[:, j % GB, :, :].rearrange("p b s -> p (b s)"),
                                        ws_hi[:, l, side, c, m * P:(m + 1) * P],
                                        ws_lo[:, l, side, c, m * P:(m + 1) * P],
                                        h_hi[n][:, c, :], h_lo[n][:, c, :], c == 0, c == HC - 1)
                last.then_inc(g_done[l], 1)

            def linear(l, q, b):
                if b == 0:
                    if at(q, 0):
                        pe.wait_ge(w_lo_done, weight_steps(3 * l + 2))
                    pl, pq = prior(l, q)
                    wait(pe, lin_sum_done[pl], QB * pq + 3)
                elif b == 1:
                    wait(pe, g_lo_done[l], NG * q + GB + 1)
                else:
                    wait(pe, lin_sum_done[l], QB * q + b - 1)
                n = own_set(l, q)
                for c in range(HC):
                    last = three_passes(lin_bank(b), h_hi[n][:, c, b * S:(b + 1) * S], h_lo[n][:, c, b * S:(b + 1) * S],
                                        wl_hi[:, l, c, :], wl_lo[:, l, c, :], c == 0, c == HC - 1)
                last.then_inc(lin_done[l], 1)

            def scores(l, q, b):
                if b == 0:
                    wait(pe, g_lo_done[l], NG * (q + 1))
                    pl, pq = prior(l, q)
                    wait(pe, u_mul_done[pl], pq + 1)
                n = own_set(l, q)
                for c in range(HC):
                    last = three_passes(ps_u[:, b, :], h_hi[n][:, c, b * S:(b + 1) * S], h_lo[n][:, c, b * S:(b + 1) * S],
                                        g_hi[:, c, b, :], g_lo[:, c, b, :], c == 0, c == HC - 1)
                last.then_inc(u_done[l], 1)

            def context(l, q, b):
                if at(q, 0) and b == 0:
                    pe.wait_ge(pads_done, 1)
                if b == 0:
                    wait(pe, p_lo_done[l], q + 1)
                wait(pe, lin_lo_done[l], QB * q + b + 1)
                if b >= 2:
                    wait(pe, y_done[l], QB * q + b - 1)
                else:
                    pl, pq = prior(l, q)
                    wait(pe, y_done[pl], QB * pq + 3 + b)
                    if b == 0 and l == 0 and at(q, 1):
                        wait(pe, relu_done, HC)
                    if b == 0 and l == 1 and at(q, NQ - 2):
                        wait(pe, relu_done, HC * NQ)
                three_passes(ctx_bank(b)[:, 0:HX], p_hi[l][:, b * S:(b + 1) * S], p_lo[l][:, b * S:(b + 1) * S],
                             lin_hi[l][:, b, :], lin_lo[l][:, b, :]).then_inc(ctx_done[l], 1)

            def transposes(q, c):
                if at(q, 0) and c == 0:
                    pe.wait_ge(const_done, 1)
                if c == 0:
                    wait(pe, z_done, QB * (q + 1))
                if c >= 2:
                    wait(pe, relu_done, HC * q + c - 1)
                for b in range(QB):
                    last = pe.transpose(ps_c[:, c % 2, b * S:(b + 1) * S], y[0][:, b, c * P:(c + 1) * P],
                                        ident[:, :])
                last.then_inc(tr_done, 1)

            def body(t):
                for j in range(NG):
                    if has(t):
                        project_sides(0, t, j)
                        if has(t - 2) and j >= 2:
                            context(1, t - 2, j - 2)
                        if at(t, 1) and j < 2:
                            context(0, 0, 2 + j)
                linear_and_scores(0, t)
                if at(t, 0):
                    context(0, 0, 0)
                    context(0, 0, 1)
                for j in range(NG):
                    if has(t - 1):
                        project_sides(1, t - 1, j)
                    if has(t) and not at(t, 0) and j >= 2:
                        context(0, t, j - 2)
                    if at(t, NQ):
                        for b in LAST_BUT_ONE[j]:
                            context(1, t - 2, b)
                linear_and_scores(1, t - 1)
                if at(t, NQ + 1):
                    for b in range(QB):
                        context(1, t - 2, b)

            def linear_and_scores(l, q):
                if not has(q):
                    return
                first = 1 if is_end(l, q) else QB
                for b in range(first):
                    linear(l, q, b)
                    if l == 0 and at(q, 1) and b < HC:
                        transposes(0, b)
                for b in range(QB):
                    scores(l, q, b)
                    if l == 1 and at(q, NQ - 2) and b < HC:
                        transposes(NQ - 1, b)
                for b in range(first, QB):
                    linear(l, q, b)

            iterations(pe, body)

        @block.scalar
        def _(act):
            def weights_hi(n):
                l, kind = n // 3, n % 3
                act.wait_ge(w_loaded[n], 16)
                dst = ws_hi[:, l, kind, :, :] if kind < 2 else wl_hi[:, l, :, :]
                nc.scalar.activation(dst.rearrange("p c n -> p (c n)"), raw_w[l][kind], ACT.Copy).then_inc(w_hi_done, 1)

            def sides_hi(l, q, j):
                side, m = j // HC, j % HC
                if j == 0:
                    pl, pq = prior(l, q)
                    wait(act, u_done[pl], QB * (pq + 1))
                wait(act, g_done[l], NG * q + j + 1)
                nc.scalar.activation(g_hi[:, m, :, side * S:(side + 1) * S], ps_g[:, j % GB, :, :],
                                     ACT.Copy).then_inc(g_hi_done[l], 1)

            def relu_affine(q, c):
                if by_tensor(q):
                    if c == 0:
                        wait(act, h_lo_done[1], HC * q)
                        if at(q, 0):
                            act.wait_ge(w_lo_done, weight_steps(3 * L - 1))
                            act.wait_ge(col_loaded, 16)
                    act.wait_ge(tr_done, tr_count(q) - HC + c + 1)
                    src = ps_c[:, c % 2, :].rearrange("p (b a i) -> p b a i", b=QB, a=NB)
                else:
                    if c == 0:
                        wait(act, z_moved, 16 * NB * NB * q)
                    src = h32_chunk(1, c)
                nc.scalar.activation(h32_chunk(1, c), src, ACT.Relu, bias=col_tab[:, 1, c:c + 1],
                                     scale=col_tab[:, 0, c:c + 1]).then_inc(relu_done, 1)

            def split_h_hi(l, q, c):
                n = own_set(l, q)
                if c == 0:
                    if n == l:
                        wait(act, u_done[l], QB * q)
                        if l == 0 and at(q, 1):
                            wait(act, lin_done[0], QB)
                    else:
                        wait(act, u_done[0], QB * NQ)
                if l == 1:
                    wait(act, relu_done, HC * q + c + 1)
                elif at(q, 0):
                    act.wait_ge(x0_loaded[c], 16)
                else:
                    wait(act, xt_loaded, 16 * q)
                nc.scalar.activation(split_chunk(h_hi[n], l, c), h32_chunk(l, c), ACT.Copy).then_inc(h_hi_done[l], 1)

            def layer1_input(q, chunks):
                for c in chunks:
                    relu_affine(q, c)
                    split_h_hi(1, q, c)

            def linear_hi(l, q, b):
                wait(act, lin_sum_done[l], QB * q + b + 1)
                if b == 0:
                    wait(act, ctx_done[l], QB * q)
                nc.scalar.activation(lin_hi[l][:, b, 0:H], lin32[:, b, :], ACT.Copy).then_inc(lin_hi_done[l], 1)

            def take_context(l, q, b):
                if b == 0:
                    if l == 0 and at(q, 1):
                        wait(act, tr_done, tr_count(0))
                    elif l == 0:
                        wait(act, turned, QB * (q - 1))
                    elif own_set(l, q) == 0:
                        wait(act, tr_done, tr_count(NQ - 1))
                    else:
                        wait(act, norm_done, q)
                    if at(q, 0):
                        act.wait_ge(w_lo_done, weight_steps(3 * L - 1))
                wait(act, ctx_done[l], QB * q + b + 1)
                nc.scalar.activation(y[own_set(l, q)][:, b, 0:H + 1], ctx_bank(b)[:, 0:H + 1],
                                     ACT.Copy).then_inc(y_done[l], 1)

            def exponentials(l, q):
                wait(act, u_mul_done[l], q + 1)
                nc.scalar.activation(score[:, :], score[:, :], ACT.Exp, scale=INV_TEMPER).then_inc(exp_done[l], 1)

            def output_norm(q):
                wait(act, nb_o_done, q + 1)
                wait(act, out_stored, 16 * q)
                ys = y[own_set(1, q)]
                for b in range(QB // 2 if is_end(1, q) else QB):
                    last = nc.scalar.activation(o_sb[:, b, :], ys[:, b, 0:H], ACT.Identity,
                                                bias=nb_o[:, b:b + 1], scale=rstd_o[:, b:b + 1])
                last.then_inc(norm_done, 1)

            def body(t):
                if has(t - 2) and not at(t, NQ + 1):
                    exponentials(1, t - 2)
                for j in range(NG):
                    if has(t):
                        sides_hi(0, t, j)
                        if has(t - 2) and j >= 2:
                            take_context(1, t - 2, j - 2)
                        if has(t - 2) and j == NG - 1:
                            layer1_input(t - 1, [0])
                        if at(t, 1) and j < 2:
                            take_context(0, 0, 2 + j)
                if at(t, 0):
                    for n in range(3, 3 * L):
                        weights_hi(n)
                    linear_hi(0, 0, 0)
                    exponentials(0, 0)
                    linear_hi(0, 0, 1)
                    linear_hi(0, 0, 2)
                    for c in range(HC):
                        split_h_hi(0, 1, c)
                    linear_hi(0, 0, 3)
                    take_context(0, 0, 0)
                    take_context(0, 0, 1)
                elif has(t):
                    for b in range(QB):
                        linear_hi(0, t, b)
                        if at(t, 1) and b < HC:
                            relu_affine(0, b)
                        elif has(t - 2) and b < HC - 1:
                            layer1_input(t - 1, [b + 1])
                if at(t, 1):
                    for c in range(HC):
                        split_h_hi(1, 0, c)
                if has(t) and not at(t, 0):
                    exponentials(0, t)
                for j in range(NG):
                    if has(t - 1):
                        sides_hi(1, t - 1, j)
                    if has(t) and has(t + 1) and not at(t, 0) and j == 1:
                        for c in range(HC):
                            split_h_hi(0, t + 1, c)
                    if has(t) and not at(t, 0) and j >= 2:
                        take_context(0, t, j - 2)
                    if at(t, NQ):
                        for b in LAST_BUT_ONE[j]:
                            take_context(1, t - 2, b)
                if has(t) and has(t - 2):
                    output_norm(t - 2)
                for b in range(QB):
                    if has(t - 1):
                        linear_hi(1, t - 1, b)
                        if at(t, NQ) and b == 0:
                            exponentials(1, t - 1)
                if at(t, NQ - 1):
                    layer1_input(t, range(HC))
                if at(t, NQ + 1):
                    for b in range(QB):
                        take_context(1, t - 2, b)
                    output_norm(t - 3)
                    output_norm(t - 2)

            for c in range(HC):
                split_h_hi(0, 0, c)
                act.wait_ge(w0_loaded[c], 16)
                nc.scalar.activation(ws_hi[:, 0, 0, c, :], raw_w[0][0][:, c * H:(c + 1) * H],
                                     ACT.Copy).then_inc(w_hi_done, 1)
            for n in range(1, 3):
                weights_hi(n)
            iterations(act, body)

        @block.vector
        def _(dve):
            def split_h_lo(l, q, c):
                n = own_set(l, q)
                wait(dve, h_hi_done[l], HC * q + c + 1)
                nc.vector.tensor_tensor(split_chunk(h_lo[n], l, c), h32_chunk(l, c), split_chunk(h_hi[n], l, c).bitcast(fp32),
                                        ALU.subtract).then_inc(h_lo_done[l], 1)

            def weights_lo(n):
                l, kind = n // 3, n % 3
                hi, lo = ((w[:, l, kind, :, :] for w in (ws_hi, ws_lo)) if kind < 2 else
                          (w[:, l, :, :] for w in (wl_hi, wl_lo)))
                dve.wait_ge(w_hi_done, weight_steps(n))
                nc.vector.tensor_tensor(lo.rearrange("p c n -> p (c n)"), raw_w[l][kind],
                                        hi.rearrange("p c n -> p (c n)").bitcast(fp32),
                                        ALU.subtract).then_inc(w_lo_done, 1)

            def sides_lo(l, q, j):
                side, m = j // HC, j % HC
                wait(dve, g_hi_done[l], NG * q + j + 1)
                cols_j = slice(side * S, (side + 1) * S)
                nc.vector.tensor_tensor(g_lo[:, m, :, cols_j], ps_g[:, j % GB, :, :],
                                        g_hi[:, m, :, cols_j].bitcast(fp32), ALU.subtract).then_inc(g_lo_done[l], 1)

            def linear_sum(l, q, b):
                if b == 0:
                    pl, pq = prior(l, q)
                    wait(dve, lin_hi_done[pl], QB * (pq + 1))
                    wait(dve, lin_lo_done[pl], QB * (pq + 1))
                    if l == 0 and at(q, 0):
                        dve.wait_ge(w_lo_done, weight_steps(1))
                        dve.wait_ge(tab_loaded, 16)
                wait(dve, lin_done[l], QB * q + b + 1)
                nc.vector.tensor_tensor(lin32[:, b, :], lin_bank(b), b_lin[l], ALU.add).then_inc(lin_sum_done[l], 1)

            def select_scores(l, q):
                wait_alone(dve, u_done[l], QB * (q + 1))
                nc.vector.copy_predicated(ps_u[:, :, 0:S], use_right[:, :, :],
                                          ps_u[:, :, S:2 * S]).then_inc(u_sel_done[l], 1)

            def mask_scores(l, q):
                wait(dve, u_sel_done[l], q + 1)
                if l == 0:
                    wait(dve, mask_done, q + 1)
                else:
                    wait(dve, masks_moved, 16 * (q + 1))
                nc.vector.tensor_tensor(score[:, :].rearrange("p (b s) -> p b s", b=QB), ps_u[:, :, 0:S],
                                        masks[l][:, 0, :].rearrange("p (b s) -> p b s", b=QB),
                                        ALU.mult).then_inc(u_mul_done[l], 1)

            def attention_full(l, q):
                wait(dve, exp_done[l], q + 1)
                nc.vector.tensor_tensor(p32[:, :], score[:, :], masks[l][:, 1, :], ALU.mult).then_inc(p_full_done[l], 1)

            def attention_parts(l, q):
                wait(dve, p_full_done[l], q + 1)
                wait(dve, ctx_done[l], QB * q)
                nc.vector.tensor_copy(p_hi[l][:, :], p32[:, :]).then_inc(p_hi_done[l], 1)
                wait(dve, p_hi_done[l], q + 1)
                nc.vector.tensor_tensor(p_lo[l][:, :], p32[:, :], p_hi[l][:, :].bitcast(fp32),
                                        ALU.subtract).then_inc(p_lo_done[l], 1)

            def layer_stats(l, q, b):
                n = own_set(l, q)
                wait(dve, y_done[l], QB * q + b + 1)
                nc.vector.bn_stats(stat[n][:, b, :], y[n][:, b, 0:H]).then_inc(stats_done[l], 1)

            def layer_moments(l, q):
                n = own_set(l, q)
                for b in range(QB):
                    wait_alone(dve, stats_done[l], QB * q + b + 1)
                    last = nc.vector.bn_aggr(mv[n][:, b, :], stat[n][:, b, :])
                last.then_inc(mv_done[l], 1)
                nc.vector.tensor_scalar(eps_s[n][:, :], y[n][:, :, H], LN_EPS, LN_EPS * SUM_EPS,
                                        ALU.mult, ALU.add).then_inc(eps_done[l], 1)

            def layer_scale(l, q):
                n = own_set(l, q)
                wait(dve, sd_done[l], q + 1)
                wait(dve, eps_done[l], q + 1)
                nc.vector.scalar_tensor_tensor(den[n][:, :], sd[n][:, :], DDOF, eps_s[n][:, :],
                                               ALU.mult, ALU.add).then_inc(den_done[l], 1)
                wait(dve, den_done[l], q + 1)
                nc.vector.reciprocal(k_ln[n][:, :], den[n][:, :]).then_inc(k_done[l], 1)

            def layer_bias(q):
                wait(dve, k_done[0], q + 1)
                nc.vector.scalar_tensor_tensor(nb_ln[:, :], mv[0][:, :, 0], -1.0, k_ln[0][:, :],
                                               ALU.mult, ALU.mult).then_inc(nb_done, 1)

            def normalise(q, bs):
                wait(dve, nb_done, q + 1)
                for b in bs:
                    nc.vector.tensor_scalar(y[0][:, b, 0:H], y[0][:, b, 0:H], k_ln[0][:, b:b + 1],
                                            nb_ln[:, b:b + 1], ALU.mult, ALU.add).then_inc(z_done, 1)

            def turn_blocks(q, bs):
                wait(dve, z_moved, 16 * NB * NB * (q - 1))
                for b in bs:
                    wait(dve, z_done, QB * q + b + 1)
                    nc.vector.transpose(z_t[:, :, :, b, :].rearrange("p f c i -> p c f i"),
                                        y[0][:, b, 0:H].rearrange("p (c f k) -> p c f k", c=HC, f=NB)).then_inc(turned, 1)

            def scale_a(q, bs):
                n = own_set(1, q)
                wait(dve, mv_done[1], q + 1)
                for b in bs:
                    nc.vector.scalar_tensor_tensor(y[n][:, b, 0:H], y[n][:, b, 0:H], mv[n][:, b, 0:1], a_row,
                                                   ALU.subtract, ALU.mult).then_inc(scale_a_done, 1)

            def affine(q, bs):
                n = own_set(1, q)
                wait(dve, k_done[1], q + 1)
                for b in bs:
                    wait(dve, scale_a_done, QB * q + b + 1)
                    nc.vector.scalar_tensor_tensor(y[n][:, b, 0:H], y[n][:, b, 0:H], k_ln[n][:, b:b + 1], b_row,
                                                   ALU.mult, ALU.add).then_inc(affine_done, 1)

            def residual(q, bs):
                n = own_set(1, q)
                wait(dve, xres_loaded, 16 * (q + 1))
                for b in bs:
                    wait(dve, affine_done, QB * q + b + 1)
                    nc.vector.scalar_tensor_tensor(y[n][:, b, 0:H], y[n][:, b, 0:H], 0.0, residual_buffer(q)[:, b, :],
                                                   ALU.max, ALU.add).then_inc(res_done, 1)

            def output_stats(q, b):
                wait(dve, res_done, QB * q + b + 1)
                nc.vector.bn_stats(stat_o[:, b, :], y[own_set(1, q)][:, b, 0:H]).then_inc(stats_o_done, 1)

            def output_moments(q):
                for b in range(QB):
                    wait_alone(dve, stats_o_done, QB * q + b + 1)
                    last = nc.vector.bn_aggr(mv_o[:, b, :], stat_o[:, b, :])
                last.then_inc(mv_o_done, 1)
                wait(dve, mv_o_done, q + 1)
                nc.vector.tensor_scalar(var_o[:, :], mv_o[:, :, 1], OUT_EPS, None, ALU.add).then_inc(var_o_done, 1)

            def output_bias(q):
                wait(dve, rstd_o_done, q + 1)
                nc.vector.scalar_tensor_tensor(nb_o[:, :], mv_o[:, :, 0], -1.0, rstd_o[:, :],
                                               ALU.mult, ALU.mult).then_inc(nb_o_done, 1)

            def linear_sums(l, q, between=()):
                for b in range(QB):
                    if has(q):
                        linear_sum(l, q, b)
                    for step, *args in between[b] if between else ():
                        step(*args)

            def body(t):
                start, end = at(t, 0), not has(t)
                old = has(t - 2)
                if old and not at(t, NQ + 1):
                    select_scores(1, t - 2)
                    if at(t, NQ):
                        split_h_lo(1, t - 1, HC - 1)
                    mask_scores(1, t - 2)
                    attention_full(1, t - 2)
                    if end:
                        attention_parts(1, t - 2)
                for j in range(NG):
                    if has(t):
                        sides_lo(0, t, j)
                        if old and j == 0:
                            attention_parts(1, t - 2)
                        if old and j >= HC:
                            layer_stats(1, t - 2, j - HC)
                        if at(t, 1):
                            for step, *args in [[], [(layer_stats, 0, 0, 0), (layer_stats, 0, 0, 1)],
                                                [(layer_stats, 0, 0, 2)], [(layer_stats, 0, 0, 3), (layer_moments, 0, 0)],
                                                [(layer_scale, 0, 0), (layer_bias, 0), (normalise, 0, range(0, 2))],
                                                [(normalise, 0, range(2, QB))]][j]:
                                step(*args)
                if has(t):
                    if start:
                        linear_sum(0, t, 0)
                        for n in range(3, 3 * L):
                            weights_lo(n)
                        select_scores(0, t)
                        mask_scores(0, t)
                        linear_sum(0, t, 1)
                        attention_full(0, t)
                        attention_parts(0, t)
                        linear_sum(0, t, 2)
                        linear_sum(0, t, 3)
                        for c in range(HC):
                            split_h_lo(0, 1, c)
                    elif old:
                        layer_stats(1, t - 2, QB - 1)
                        linear_sums(0, t, [[(layer_moments, 1, t - 2)], [(scale_a, t - 2, range(0, 2))],
                                           [(scale_a, t - 2, range(2, QB))], [(layer_scale, 1, t - 2)]])
                        affine(t - 2, range(QB))
                        residual(t - 2, range(2))
                    else:
                        linear_sums(0, t)
                        for c in range(HC):
                            split_h_lo(1, 0, c)
                if has(t) and not start:
                    select_scores(0, t)
                    mask_scores(0, t)
                    if old:
                        residual(t - 2, range(2, QB))
                    attention_full(0, t)
                for j in range(NG):
                    if has(t - 1):
                        sides_lo(1, t - 1, j)
                    if has(t):
                        if j == 0 and not start:
                            attention_parts(0, t)
                        if old and j >= 1 and j <= QB:
                            output_stats(t - 2, j - 1)
                        if not start and j >= HC:
                            layer_stats(0, t, j - HC)
                        if old and j == QB:
                            output_moments(t - 2)
                    elif at(t, NQ) and j > 0:
                        for b in LAST_BUT_ONE[j - 1]:
                            layer_stats(1, t - 2, b)
                if has(t) and not start:
                    layer_stats(0, t, QB - 1)
                    linear_sums(1, t - 1, [[(layer_moments, 0, t)] + ([(output_bias, t - 2)] if old else []),
                                           [(layer_scale, 0, t), (layer_bias, t), (normalise, t, range(0, 2))],
                                           [(normalise, t, range(2, QB))],
                                           [] if by_tensor(t) else [(turn_blocks, t, range(QB))]])
                    if at(t, NQ - 1):
                        for c in range(HC - 1):
                            split_h_lo(1, t, c)
                elif at(t, NQ):
                    layer_moments(1, t - 2)
                    linear_sum(1, t - 1, 0)
                    scale_a(t - 2, range(QB))
                    layer_scale(1, t - 2)
                    affine(t - 2, range(3))
                    select_scores(1, t - 1)
                    mask_scores(1, t - 1)
                    linear_sum(1, t - 1, 1)
                    affine(t - 2, range(3, QB))
                    attention_full(1, t - 1)
                    attention_parts(1, t - 1)
                    linear_sum(1, t - 1, 2)
                    linear_sum(1, t - 1, 3)
                    residual(t - 2, range(QB))
                    for b in range(QB):
                        output_stats(t - 2, b)
                    output_moments(t - 2)
                elif at(t, NQ + 1):
                    for b in range(QB):
                        layer_stats(1, t - 2, b)
                    layer_moments(1, t - 2)
                    output_bias(t - 3)
                    scale_a(t - 2, range(QB))
                    layer_scale(1, t - 2)
                    for b in range(QB):
                        affine(t - 2, [b])
                        residual(t - 2, [b])
                        if b > 0:
                            output_stats(t - 2, b - 1)
                    output_stats(t - 2, QB - 1)
                    output_moments(t - 2)
                    output_bias(t - 2)
                    dve.wait_ge(nb_o_done, NQ)
                    dve.wait_ge(out_stored, 16 * (NQ - 1))
                    for b in range(QB // 2, QB):
                        last = nc.vector.tensor_scalar(o_sb[:, b, :], y[0][:, b, 0:H], rstd_o[:, b:b + 1],
                                                       nb_o[:, b:b + 1], ALU.mult, ALU.add)
                    last.then_inc(last_half_done, 1)

            for l in range(L):
                nc.vector.memset(lin_hi[l][:, :, H:H + 1].bitcast(fp32), 1.0)
                nc.vector.memset(lin_hi[l][:, :, H + 1:HX].bitcast(fp32), 0.0)
                last = nc.vector.memset(lin_lo[l][:, :, H:HX].bitcast(fp32), 0.0)
            last.then_inc(pads_done, 1)
            dve.wait_ge(const_done, 1)
            for c in range(HC):
                split_h_lo(0, 0, c)
                dve.wait_ge(w_hi_done, c + 1)
                nc.vector.tensor_tensor(ws_lo[:, 0, 0, c, :], raw_w[0][0][:, c * H:(c + 1) * H],
                                        ws_hi[:, 0, 0, c, :].bitcast(fp32), ALU.subtract).then_inc(w_lo_done, 1)
            for n in range(1, 3):
                weights_lo(n)
            iterations(dve, body)

        @block.gpsimd
        def _(pool):
            def low_part(lo, full, hi):
                return nc.gpsimd.tensor_tensor(lo, full, hi.bitcast(fp32), ALU.subtract)

            def split_h_lo(l, q, chunks=range(HC)):
                if is_edge(l, q):
                    return
                for c in chunks:
                    wait(pool, h_hi_done[l], HC * q + c + 1)
                    low_part(split_chunk(h_lo[l], l, c), h32_chunk(l, c), split_chunk(h_hi[l], l, c)).then_inc(h_lo_done[l], 1)

            def linear_lo(l, q):
                for b in range(QB):
                    wait(pool, lin_hi_done[l], QB * q + b + 1)
                    low_part(lin_lo[l][:, b, 0:H], lin32[:, b, :], lin_hi[l][:, b, 0:H]).then_inc(lin_lo_done[l], 1)

            def deviation(l, q):
                n = own_set(l, q)
                wait(pool, mv_done[l], q + 1)
                nc.gpsimd.tensor_tensor(sd[n][:, :], mv[n][:, :, 1], halves[:, 0, :], ALU.pow).then_inc(sd_done[l], 1)

            def make_masks(q):
                wait_alone(pool, adj_loaded, 32 * (q + 1))
                nc.gpsimd.affine_select(out=adj_nat[:, :], in_=adj_nat[:, :], compare_op=ALU.is_gt, fill=0.0,
                                        base=0, pattern=[[0, QB], [1, S]], channel_multiplier=-1).then_inc(mask_step, 1)
                nc.gpsimd.affine_select(out=masks[0][:, 0, :], in_=masks[0][:, 1, :], compare_op=ALU.is_ge, fill=0.0,
                                        base=0, pattern=[[0, QB], [-1, S]], channel_multiplier=1).then_inc(mask_step, 1)
                wait(pool, mask_step, 2 * (q + 1))
                nc.gpsimd.tensor_tensor(masks[0][:, 0, :], masks[0][:, 0, :], adj_nat[:, :],
                                        ALU.add).then_inc(mask_done, 1)

            def output_rstd(q):
                wait(pool, var_o_done, q + 1)
                wait(pool, norm_done, q)
                nc.gpsimd.tensor_tensor(rstd_o[:, :], var_o[:, :], halves[:, 1, :], ALU.pow).then_inc(rstd_o_done, 1)

            def body(t):
                if has(t - 1):
                    split_h_lo(1, t - 1, range(2))
                if has(t) and has(t - 2):
                    deviation(1, t - 2)
                if has(t - 1):
                    split_h_lo(1, t - 1, range(2, HC))
                if has(t) and not at(t, 0):
                    make_masks(t)
                if has(t):
                    linear_lo(0, t)
                if has(t) and has(t + 1):
                    split_h_lo(0, t + 1)
                if has(t) and has(t - 2):
                    output_rstd(t - 2)
                if has(t):
                    deviation(0, t)
                if at(t, NQ):
                    deviation(1, t - 2)
                if has(t - 1):
                    linear_lo(1, t - 1)
                if at(t, NQ):
                    output_rstd(t - 2)
                if at(t, NQ + 1):
                    deviation(1, t - 2)
                    output_rstd(t - 2)

            nc.gpsimd.memset(ident[:, :], 0.0).then_inc(const_step, 1)
            nc.gpsimd.memset(use_right[:, :, :], 1).then_inc(const_step, 1)
            nc.gpsimd.memset(halves[:, 0, :], 0.5).then_inc(const_step, 1)
            nc.gpsimd.memset(halves[:, 1, :], -0.5).then_inc(const_step, 1)
            pool.wait_ge(const_step, 4)
            nc.gpsimd.affine_select(out=ident[:, :], in_=ident[:, :], compare_op=ALU.not_equal, fill=1.0, base=0,
                                    pattern=[[-1, P]], channel_multiplier=1).then_inc(const_step, 1)
            nc.gpsimd.affine_select(out=use_right[:, :, :], in_=use_right[:, :, :], compare_op=ALU.is_gt, fill=0.0,
                                    base=0, pattern=[[0, QB], [1, S]], channel_multiplier=-1).then_inc(const_step, 1)
            pool.wait_ge(const_step, 6)
            nc.gpsimd.memset(var_o[:, :], 0.0).then_inc(const_done, 1)
            make_masks(0)
            iterations(pool, body)


_OUT = ((128, 128, 384), "float32")


def kernel(**inputs):
    import concourse.bacc as _bacc
    from concourse.bass_utils import run_bass_kernel_spmd as _run

    P, QB = 128, 4
    v = {n: np.asarray(a) for n, a in inputs.items()}
    x, adj = v["x"], v["adj"]
    B, S, H = x.shape
    NQ, HC = B // QB, H // P

    x_t = x.reshape(NQ, QB, S, HC, P).transpose(0, 4, 3, 1, 2).reshape(NQ, P, HC * QB * S)
    a4 = adj.reshape(NQ, QB, S, S)
    adj_pair = np.stack([a4.transpose(0, 2, 1, 3), a4.transpose(0, 3, 1, 2)], axis=2).reshape(NQ, S, 2, QB * S)
    w_side = np.stack([v["L0_gnn_W_left"], v["L0_gnn_W_right"]], axis=1)
    w_lin_t = v["L0_gnn_W_lin"].transpose(0, 2, 1)
    b_lin, ln_a, ln_b = v["L0_gnn_b_lin"], v["L0_gnn_ln_a"], v["L0_gnn_ln_b"]
    rows = np.broadcast_to(np.stack([b_lin[0], b_lin[1], ln_a[1], ln_b[1]])[None], (P, 4, H))
    cols = np.stack([ln_a[0].reshape(HC, P), ln_b[0].reshape(HC, P)]).transpose(2, 0, 1)

    nc = _bacc.Bacc("TRN2", target_bir_lowering=False, num_devices=1)
    arrays, args = {}, []
    for name, a in (("x_nat", x), ("x_t", x_t), ("adj_pair", adj_pair), ("w_side", w_side),
                    ("w_lin_t", w_lin_t), ("rows", rows), ("cols", cols)):
        a = np.ascontiguousarray(a)
        arrays[name] = a
        args.append(nc.dram_tensor(name, a.shape, mybir.dt.from_np(a.dtype), kind="ExternalInput").ap())
    out = nc.dram_tensor("out", _OUT[0], mybir.dt.float32, kind="ExternalOutput").ap()
    gnn_attention_resnorm_kernel(nc, *args, out)
    r = _run(nc, [arrays], core_ids=[0])
    return r.results[0]["out"]
```
